# Optimizing a Trainium2 kernel written in Bass

```python
import numpy as np
import jax
import jax.numpy as jnp

def _softmax(x, axis=-1):
    return jax.nn.softmax(x, axis=axis)

def _gelu(x):
    return jax.nn.gelu(x, approximate=True)

def _silu(x):
    return jax.nn.silu(x)

def _sigmoid(x):
    return jax.nn.sigmoid(x)

def _layernorm(x, axis=-1, eps=1e-05):
    m = jnp.mean(x, axis=axis, keepdims=True)
    v = jnp.var(x, axis=axis, keepdims=True)
    return (x - m) / jnp.sqrt(v + eps)

def _scatter_add(tgt, idx, src, axis=0):
    return tgt.at[idx].add(src)

def _segment_sum(src, seg, n):
    return jax.ops.segment_sum(src, seg, n)
kernel_name = 'mk_audio_tower_d1_tok_audfeat1024_r4_2a93ec'

def setup_inputs(seed: int=0):
    np.random.seed(seed)
    _w = jnp.asarray

    def _rec_inputs():
        import jax
        import jax.numpy as jnp
        _rk = jax.random.key(seed)
        x = 7.22013e-05 + 1.00017 * jax.random.normal(jax.random.fold_in(_rk, 1), (16, 750, 128), jnp.float32)
        return x
    x = _rec_inputs()

    def _L0_tok_setup():
        import jax, jax.numpy as jnp
        import numpy as np
        K = 2
        H = 8
        D_LLM = 256
        DK = D_LLM // H
        N_LAYER = 2
        F_HID = D_LLM // 4
        EPS = 1e-12

        def _ln(x, g, b):
            m = jnp.mean(x, axis=-1, keepdims=True)
            v = jnp.mean((x - m) ** 2, axis=-1, keepdims=True)
            return (x - m) * jax.lax.rsqrt(v + EPS) * g + b
        key = jax.random.key(seed)
        ks = jax.random.split(key, 16)
        s = 0.02
        d_in = 128 * K
        d_ff = 512
        inp = {'x': jax.random.normal(ks[0], (8, 512, 128), dtype=jnp.float32), 'W1': jax.random.normal(ks[1], (d_ff, d_in)) * s, 'b1': jnp.zeros((d_ff,)), 'W2': jax.random.normal(ks[2], (D_LLM, d_ff)) * s, 'b2': jnp.zeros((D_LLM,)), 'ln1_g': jnp.ones((N_LAYER, D_LLM)), 'ln1_b': jnp.zeros((N_LAYER, D_LLM)), 'ln2_g': jnp.ones((N_LAYER, D_LLM)), 'ln2_b': jnp.zeros((N_LAYER, D_LLM)), 'Wq': jax.random.normal(ks[3], (N_LAYER, D_LLM, D_LLM)) * s, 'bq': jnp.zeros((N_LAYER, D_LLM)), 'Wk': jax.random.normal(ks[4], (N_LAYER, D_LLM, D_LLM)) * s, 'bk': jnp.zeros((N_LAYER, D_LLM)), 'Wv': jax.random.normal(ks[5], (N_LAYER, D_LLM, D_LLM)) * s, 'bv': jnp.zeros((N_LAYER, D_LLM)), 'Wo': jax.random.normal(ks[6], (N_LAYER, D_LLM, D_LLM)) * s, 'bo': jnp.zeros((N_LAYER, D_LLM)), 'Fw1': jax.random.normal(ks[7], (N_LAYER, F_HID, D_LLM)) * s, 'Fb1': jnp.zeros((N_LAYER, F_HID)), 'Fw2': jax.random.normal(ks[8], (N_LAYER, D_LLM, F_HID)) * s, 'Fb2': jnp.zeros((N_LAYER, D_LLM))}
        return inp
    _L0_tok_all = _L0_tok_setup()
    _L0_tok_in = {k: v for k, v in _L0_tok_all.items() if k in ('W1', 'b1', 'W2', 'b2', 'ln1_g', 'ln1_b', 'ln2_g', 'ln2_b', 'Wq', 'bq', 'Wk', 'bk', 'Wv', 'bv', 'Wo', 'bo', 'Fw1', 'Fb1', 'Fw2', 'Fb2')}
    del _L0_tok_all

    def _L0_attn_setup():
        import jax, jax.numpy as jnp
        import numpy as np
        NUM_HEADS = 16
        N_EMBD = 256

        def alibi_bias(num_heads: int, seq_len: int) -> jnp.ndarray:
            pos = jnp.arange(seq_len, dtype=jnp.float32)
            dgrid = pos[None, :] - pos[:, None]
            slopes = 2.0 ** (-8.0 / num_heads * (jnp.arange(num_heads, dtype=jnp.float32) + 1.0))
            bias = slopes[:, None, None] * dgrid[None, :, :]
            return jnp.where(dgrid[None, :, :] > 0, -jnp.inf, bias)
        key = jax.random.key(seed)
        k1, k2, k3 = jax.random.split(key, 3)
        B, L, E = (2, 512, N_EMBD)
        x = jax.random.normal(k1, (B, L, E), dtype=jnp.float32)
        w_in = jax.random.normal(k2, (3 * E, E), dtype=jnp.float32) * 0.02
        w_out = jax.random.normal(k3, (E, E), dtype=jnp.float32) * 0.02
        return {'x': x, 'w_in': w_in, 'w_out': w_out}
    _L0_attn_all = _L0_attn_setup()
    _L0_attn_in = {k: v for k, v in _L0_attn_all.items() if k in ('w_in', 'w_out')}
    del _L0_attn_all

    def _L0_ffn_setup():
        import jax, jax.numpy as jnp
        import numpy as np
        B, S, H, E = (2, 2048, 256, 8)
        SCALE = 0.5
        key = jax.random.key(seed)
        k1, k2 = jax.random.split(key)
        x = jax.random.normal(k1, (B, S, H), dtype=jnp.float32)
        gate_w = jax.random.normal(k2, (E, H), dtype=jnp.float32) * 0.02
        coeff = SCALE * (1.0 + 0.05 * jnp.arange(E, dtype=jnp.float32))
        expert_w = coeff[:, None, None] * jnp.eye(H, dtype=jnp.float32)
        return {'x': x, 'gate_w': gate_w, 'expert_w': expert_w}
    _L0_ffn_all = _L0_ffn_setup()
    _L0_ffn_in = {k: v for k, v in _L0_ffn_all.items() if k in ('gate_w', 'expert_w')}
    del _L0_ffn_all
    return {'x': x, 'L0_tok_W1': _L0_tok_in['W1'], 'L0_tok_b1': _L0_tok_in['b1'], 'L0_tok_W2': _L0_tok_in['W2'], 'L0_tok_b2': _L0_tok_in['b2'], 'L0_tok_ln1_g': _L0_tok_in['ln1_g'], 'L0_tok_ln1_b': _L0_tok_in['ln1_b'], 'L0_tok_ln2_g': _L0_tok_in['ln2_g'], 'L0_tok_ln2_b': _L0_tok_in['ln2_b'], 'L0_tok_Wq': _L0_tok_in['Wq'], 'L0_tok_bq': _L0_tok_in['bq'], 'L0_tok_Wk': _L0_tok_in['Wk'], 'L0_tok_bk': _L0_tok_in['bk'], 'L0_tok_Wv': _L0_tok_in['Wv'], 'L0_tok_bv': _L0_tok_in['bv'], 'L0_tok_Wo': _L0_tok_in['Wo'], 'L0_tok_bo': _L0_tok_in['bo'], 'L0_tok_Fw1': _L0_tok_in['Fw1'], 'L0_tok_Fb1': _L0_tok_in['Fb1'], 'L0_tok_Fw2': _L0_tok_in['Fw2'], 'L0_tok_Fb2': _L0_tok_in['Fb2'], 'L0_attn_w_in': _L0_attn_in['w_in'], 'L0_attn_w_out': _L0_attn_in['w_out'], 'L0_ffn_gate_w': _L0_ffn_in['gate_w'], 'L0_ffn_expert_w': _L0_ffn_in['expert_w']}

def reference(x, L0_tok_W1, L0_tok_b1, L0_tok_W2, L0_tok_b2, L0_tok_ln1_g, L0_tok_ln1_b, L0_tok_ln2_g, L0_tok_ln2_b, L0_tok_Wq, L0_tok_bq, L0_tok_Wk, L0_tok_bk, L0_tok_Wv, L0_tok_bv, L0_tok_Wo, L0_tok_bo, L0_tok_Fw1, L0_tok_Fb1, L0_tok_Fw2, L0_tok_Fb2, L0_attn_w_in, L0_attn_w_out, L0_ffn_gate_w, L0_ffn_expert_w):
    import jax
    import jax.numpy as jnp

    def _L0_tok_ref(x, W1, b1, W2, b2, ln1_g, ln1_b, ln2_g, ln2_b, Wq, bq, Wk, bk, Wv, bv, Wo, bo, Fw1, Fb1, Fw2, Fb2):
        import jax, jax.numpy as jnp
        import numpy as np
        K = 2
        H = 8
        D_LLM = 256
        DK = D_LLM // H
        N_LAYER = 2
        F_HID = D_LLM // 4
        EPS = 1e-12

        def _ln(x, g, b):
            m = jnp.mean(x, axis=-1, keepdims=True)
            v = jnp.mean((x - m) ** 2, axis=-1, keepdims=True)
            return (x - m) * jax.lax.rsqrt(v + EPS) * g + b
        B, S, D = x.shape
        chunk = (S - 1) // K + 1
        pad = chunk * K - S
        x = jnp.pad(x, ((0, 0), (0, pad), (0, 0)))
        x = x.reshape(B, chunk, K * D)
        x = jax.nn.relu(x @ W1.T + b1) @ W2.T + b2
        T = chunk
        for l in range(N_LAYER):
            resid = x
            h = _ln(x, ln1_g[l], ln1_b[l])
            q = (h @ Wq[l].T + bq[l]).reshape(B, T, H, DK).transpose(0, 2, 1, 3)
            k_ = (h @ Wk[l].T + bk[l]).reshape(B, T, H, DK).transpose(0, 2, 1, 3)
            v = (h @ Wv[l].T + bv[l]).reshape(B, T, H, DK).transpose(0, 2, 1, 3)
            scores = jnp.einsum('bhqd,bhkd->bhqk', q, k_) * DK ** (-0.5)
            attn = jax.nn.softmax(scores, axis=-1)
            o = jnp.einsum('bhqk,bhkd->bhqd', attn, v)
            o = o.transpose(0, 2, 1, 3).reshape(B, T, H * DK)
            x = resid + o @ Wo[l].T + bo[l]
            resid = x
            h = _ln(x, ln2_g[l], ln2_b[l])
            x = resid + jax.nn.relu(h @ Fw1[l].T + Fb1[l]) @ Fw2[l].T + Fb2[l]
        return x

    def _L0_attn_ref(x, w_in, w_out):
        import jax, jax.numpy as jnp
        import numpy as np
        NUM_HEADS = 16
        N_EMBD = 256

        def alibi_bias(num_heads: int, seq_len: int) -> jnp.ndarray:
            pos = jnp.arange(seq_len, dtype=jnp.float32)
            dgrid = pos[None, :] - pos[:, None]
            slopes = 2.0 ** (-8.0 / num_heads * (jnp.arange(num_heads, dtype=jnp.float32) + 1.0))
            bias = slopes[:, None, None] * dgrid[None, :, :]
            return jnp.where(dgrid[None, :, :] > 0, -jnp.inf, bias)
        B, L, E = x.shape
        H = NUM_HEADS
        D = E // H
        qkv = jnp.einsum('ble,fe->blf', x, w_in)
        q, k, v = jnp.split(qkv, 3, axis=-1)

        def to_heads(t):
            return t.reshape(B, L, H, D).transpose(0, 2, 1, 3)
        q, k, v = (to_heads(q), to_heads(k), to_heads(v))
        scale = 1.0 / jnp.sqrt(jnp.asarray(D, dtype=x.dtype))
        scores = jnp.einsum('bhqd,bhkd->bhqk', q, k) * scale
        scores = scores + alibi_bias(H, L)[None]
        attn = jax.nn.softmax(scores, axis=-1)
        ctx = jnp.einsum('bhqk,bhkd->bhqd', attn, v)
        ctx = ctx.transpose(0, 2, 1, 3).reshape(B, L, E)
        return jnp.einsum('ble,fe->blf', ctx, w_out)

    def _L0_ffn_ref(x, gate_w, expert_w):
        import jax, jax.numpy as jnp
        import numpy as np
        B, S, H, E = (2, 2048, 256, 8)
        SCALE = 0.5
        scores = jnp.einsum('bsh,eh->bse', x, gate_w)
        chosen = jnp.argmax(scores, axis=-1)
        onehot = jax.nn.one_hot(chosen, gate_w.shape[0], dtype=x.dtype)
        expert_out = jnp.einsum('bsh,efh->bsef', x, expert_w)
        return x + jnp.einsum('bsef,bse->bsf', expert_out, onehot)
    h = _L0_tok_ref(x, L0_tok_W1, L0_tok_b1, L0_tok_W2, L0_tok_b2, L0_tok_ln1_g, L0_tok_ln1_b, L0_tok_ln2_g, L0_tok_ln2_b, L0_tok_Wq, L0_tok_bq, L0_tok_Wk, L0_tok_bk, L0_tok_Wv, L0_tok_bv, L0_tok_Wo, L0_tok_bo, L0_tok_Fw1, L0_tok_Fb1, L0_tok_Fw2, L0_tok_Fb2)
    h = h + _L0_attn_ref(_layernorm(h, axis=-1), L0_attn_w_in, L0_attn_w_out)
    h = h + _L0_ffn_ref(_layernorm(h, axis=-1), L0_ffn_gate_w, L0_ffn_expert_w)
    return h

_drawn_inputs = setup_inputs


def setup_inputs(seed=0):
    import zlib

    import numpy as np

    out = dict(_drawn_inputs(seed))
    spreads = {'L0_tok_b1': (0.0, 0.1),
     'L0_tok_b2': (0.0, 0.1),
     'L0_tok_ln1_g': (1.0, 0.2),
     'L0_tok_ln1_b': (0.0, 0.1),
     'L0_tok_ln2_g': (1.0, 0.2),
     'L0_tok_ln2_b': (0.0, 0.411),
     'L0_tok_bq': (0.0, 0.8),
     'L0_tok_bk': (0.0, 0.8),
     'L0_tok_bv': (0.0, 0.1),
     'L0_tok_bo': (0.0, 0.1),
     'L0_tok_Fb1': (0.0, 0.1),
     'L0_tok_Fb2': (0.0, 0.1)}
    factors = {'L0_tok_Wq': 8.0, 'L0_tok_Wk': 8.0}
    for name, (base, spread) in spreads.items():
        noise = np.random.default_rng([zlib.crc32(name.encode()), seed]).standard_normal(out[name].shape)
        drawn = base * np.exp(spread * noise) if base else spread * noise
        out[name] = jnp.asarray(drawn.astype(out[name].dtype))
    for name, factor in factors.items():
        out[name] = (out[name] * factor).astype(out[name].dtype)
    return out
```

```python
from contextlib import ExitStack

import numpy as np
import concourse.bass as bass
from concourse import mybir

F32 = mybir.dt.float32
F32R = mybir.dt.float32r
BF16 = mybir.dt.bfloat16
ALU = mybir.AluOpType
ACT = mybir.ActivationFunctionType
AX = mybir.AxisListType

NB, S, DIN = 16, 750, 128
T = S // 2
TP = T + 1
TT = 125
NT = T // TT
D = 256
KT = D // 128
DFF, FH = 512, 64
MT = DFF // 128
NE = 8
EPS_TOK, EPS_FIN = 1e-12, 1e-5
MASKED = -1e30
EXP_LN_SET = 6
NCONST = 25
LANES = 2
TURNS = NB // LANES
FIN = 2
HD = {0: 32, 1: 32, FIN: 16}
GROUPS = {0: 2, 1: 2, FIN: 4}
MROW = 96
SCALE = {0: 32 ** -0.5, 1: 32 ** -0.5, FIN: 16 ** -0.5}

WCOL = {}
_at = 0
for _name, _kt, _n, _rows in (
        [("W1", KT, DFF, 128), ("W2", MT, D, 128)]
        + [x for n in (0, 1) for x in ((f"qkv{n}", KT, 3 * D, 128), (f"o{n}", KT, D, 128),
                                       (f"f1{n}", KT, FH, 128), (f"f2{n}", 1, D, FH))]
        + [("qkv2", KT, 3 * D, 128), ("o2", KT, D, 128), ("gate", KT, NE, 128),
           ("exp", KT, NE * D, 128)]):
    WCOL[_name] = (_at, _kt, _n, _rows)
    _at += _kt * _n
WCOLS = _at


OWNER = {
    "g_full": "pe",
    "s_full": "pe", "t_full": "pe",
    "o_full": "pe",
    "s_max": "dve",
    "exp": "act",
    "causal": "pool",
    "x_in0": "sp", "x_in1": "sp", "x_hi": "act", "x_lo": "pool",
    "r_done": "dve", "r_hi": "act", "r_lo": "pool",
    "hi": "act", "lo": "dve",
    "v_done": "dve", "vf_done": "act", "v_zero": "pool",
    "x_done": "dve",
    "scr0": "sp", "scr1": "sp",
    "st_in0": "sp", "st_in1": "sp",
    "nm_row": "act",
    "ln_st": "dve", "ln_mv": "dve", "ln_log": "act", "ln_rstd": "act", "h_done": "dve",
    "x_bias": "pool", "z_done": "pool",
    "gate": "dve", "hot": "dve", "den": "act", "out0": "sp", "out1": "sp"}


def lane_steps(l):
    out = []

    def add(step, *needs):
        out.append((step, needs))
        return step

    p = add(("xin", l))
    for m in range(MT):
        h = add(("up", l, m), p)
    for i in range(NT):
        p = add(("down", l, i), h)
    p = add(("lnv", l, 0, 0), p)
    for n in (0, 1, FIN):
        p = add(("lnt", l, n, 0), p)
        for m in range(4):
            q = add(("qkv", l, n, m), p)
        s = add(("spill", l, n), q)
        for i in range(NT):
            v = add(("qkv", l, n, 4 + i), p)
        for g in range(GROUPS[n]):
            u = (l, n, g)
            f = add(("fill", u), s)
            for j in range(4):
                m = add(("S", u, j), f)
            m = add(("nm", u), m)
            for kt in range(NT):
                t = add(("T", u, kt), m)
                pv = add(("pv", u, kt), t, v)
            if n != FIN or g % 2:
                o = add(("norm", u), pv)
        if n == FIN:
            add(("xload", l), pv)
        for i in range(NT):
            p = add(("wo", l, n, i), o)
        p = add(("lnv", l, n, 1), p)
        p = add(("lnt", l, n, 1), p)
        if n != FIN:
            p = add(("f1", l, n), p)
            for i in range(NT):
                h = add(("f2", l, n, i), p)
            p = add(("lnv", l, n + 1, 0), h)
    p = add(("gate", l), p)
    for i in range(NT):
        for e in range(NE // 2):
            h = add(("moe", l, i, e), p)
    add(("out", l), h)
    return out


def cost(step):
    k = step[0]
    fin = (step[1][1] if isinstance(step[1], tuple) else step[2] if len(step) > 2 else 0) == FIN
    if k == "qkv":
        return (1.0, ("act", .4), ("dve", .5)) if step[3] < 4 else (.65, ("act", .7) if fin else ("dve", .4))
    return {"xin": (0, ("act", .8), ("pool", 1.8)), "up": (1.0, ("dve", .5), ("act", .4), ("pool", .9)),
            "down": (1.3, ("dve", .35)), "lnv": (0, ("dve", 1.6), ("act", .6), ("dve", 1.0), ("pool", 1.7)),
            "lnt": (1.3, ("act", .8), ("dve", .9)), "spill": (0, ("sp", 1.3), ("dma", 3.0)),
            "fill": (0, ("sp", 4.0 if fin else 3.0), ("dma", 2.5)),
            "S": (.75, ("dve", 1.15)) if fin else (.6, ("dve", 1.5)), "nm": (.25, ("act", .8)),
            "T": (.75, ("act", 1.2), ("pool", .8)) if fin else (.75, ("act", 1.7)),
            "pv": (1.5 if fin else 2.1,), "norm": (0, ("act", .9), ("dve", .5), ("act", .45), ("pool", .9)),
            "xload": (0, ("sp", .5)), "wo": (.65, ("dve", .35)), "f1": (1.0, ("dve", .5), ("act", .4), ("pool", .9)),
            "f2": (.35, ("dve", .35)), "gate": (.6, ("dve", 1.2)), "moe": (1.3, ("dve", .75)),
            "out": (0, ("sp", .7))}[k]


CUT = ("moe", 1, 0, 0)


def order():
    lanes = [lane_steps(0), lane_steps(1)]
    at = [s for s, _ in lanes[1]].index(CUT)
    late = {s for s, _ in lanes[1][at:]}
    lanes[1] = lanes[1][at:] + lanes[1][:at]
    needs, behind, tracks = {}, {}, {}
    for l, steps in enumerate(lanes):
        names = [s for s, _ in steps]
        for p, (s, need) in enumerate(steps):
            needs[s] = [x for x in need if names.index(x) < p]
            if s[0] == "xin" and p:
                needs[s] = [names[p - 1]]
            tracks.setdefault((l, {"fill": "s", "S": "s", "nm": "s", "T": "t", "pv": "t"}.get(s[0])), []).append(s)
        load = 0
        for s in reversed(names):
            load += W_LOAD * cost(s)[0]
            behind[s] = max(load, sum([cost(s)[0]] + [d for _, d in cost(s)[1:]]) + max(
                [behind[x] for x in behind if s in needs[x]], default=0))
    free = dict(pe=0, act=0, dve=0, pool=0, sp=0)
    bank, s_done, t_done = [0, 0], 0, 0
    done, units, out = {}, [], []

    def start(s):
        k, u = s[:2]
        wait = list(needs[s])
        if any(x not in done for x in wait):
            return None
        if k == "fill" and units:
            v = units[-1]
            if v[1] == FIN and v[2] % 2 == 0 and u != (v[0], FIN, v[2] + 1):
                return None
            if len(units) > 1:
                wait.append(("T", units[-2], NT - 1))
        if k in ("T", "pv") and units.index(u):
            v = units[units.index(u) - 1]
            if k == "T":
                wait.append(("pv", v, s[2]))
            elif s[2] == 0 and ("norm", v) in needs:
                wait.append(("norm", v))
        if any(x not in done for x in wait):
            return None
        t = max([done[x] - (1.4 if x[0] == "norm" and k == "pv" else 0) for x in wait], default=0)
        if cost(s)[0]:
            t = max(t, free["pe"], s_done - .9 if k == "S" else t_done - .8 if k == "T" else 0 if k == "pv"
                    else bank[0])
        return t

    while any(tracks.values()):
        ready = [(start(q[0]), q) for q in tracks.values() if q and start(q[0]) is not None]
        first = min(t for t, _ in ready)
        t, q = min(((t, q) for t, q in ready if t <= first + .1), key=lambda x: -behind[x[1][0]])
        s = q.pop(0)
        k, (pe, *rest) = s[0], cost(s)
        end = freed = t + pe
        for n, (e, d) in enumerate(rest):
            begin = t + .3 if k in ("S", "T") and n == 0 else end
            end = max(begin, free.get(e, 0)) + d
            if e != "dma":
                free[e] = end
            if n == 0 and k in ("S", "T"):
                freed = max(freed, end - (.9 if k == "S" else .8))
                s_done, t_done = (end, t_done) if k == "S" else (s_done, end)
        if pe:
            free["pe"] = freed
            if k not in ("S", "T", "pv"):
                bank = [bank[1], freed + .5 if k in ("up", "f1") else end]
        if k == "fill":
            units.append(s[1])
        done[s] = end
        out.append(s)
    return out, late


W_LOAD = 1.6
ORDER, LATE = order()


class Count:

    def __init__(self):
        self.total, self.after, self.spot, self.by_step = 0, {}, {}, {}

    def add(self, key, n, spot, step):
        self.total += n
        self.after[key], self.spot[key] = self.total, spot
        self.by_step[step] = self.by_step.get(step, 0) + n


def tower_kernel(nc, xT, w, small, alibi_q, alibi_k, out):
    with ExitStack() as ctx:
        def sb(name, shape, dt):
            return ctx.enter_context(nc.sbuf_tensor(name, shape, dt))

        def bank(name):
            return ctx.enter_context(nc.psum_tensor(name, [128, 512], F32))

        def sem(name):
            return ctx.enter_context(nc.semaphore(name))

        w_hi, w_lo = sb("w_hi", [128, WCOLS], F32R), sb("w_lo", [128, WCOLS], F32R)
        xres = [sb(f"xres{l}", [128, NT, D], F32) for l in range(LANES)]
        hv = [sb(f"hv{l}", [128, 6 * D], F32) for l in range(LANES)]
        a_hi = [sb(f"a_hi{l}", [128, KT, TP], F32R) for l in range(LANES)]
        a_lo = [sb(f"a_lo{l}", [128, KT, TP], F32R) for l in range(LANES)]
        b_hi = [sb(f"b_hi{l}", [128, MT, TP], F32R) for l in range(LANES)]
        b_lo = [sb(f"b_lo{l}", [128, MT, TP], F32R) for l in range(LANES)]
        q_st = [sb(f"q_st{s}", [128, 4, TP], F32R) for s in range(2)]
        k_st = [sb(f"k_st{s}", [128, 4, TP], F32R) for s in range(2)]
        pt = sb("pt", [128, 4, NT, TP], F32)
        rt = [sb(f"rt{s}", [128, TP], F32) for s in range(2)]
        lden = sb("lden", [128, T], F32)
        rden = sb("rden", [128, T], F32)
        nmx = [sb(f"nmx{s}", [128, 12], F32) for s in range(2)]
        scr = [[nc.dram_tensor(f"scr{l}{x}", [128, MT, TP], F32, kind="Internal").ap() for x in ("hi", "lo")]
               for l in range(LANES)]
        ali_q = nc.dram_tensor("ali_q", [64, T], F32, kind="Internal").ap()
        ali_k = nc.dram_tensor("ali_k", [MROW - 48, T], F32, kind="Internal").ap()
        stats = sb("stats", [128, LANES, NT, 6], F32)
        mv = sb("mv", [128, LANES, NT, 2], F32)
        lnv_t = sb("lnv_t", [128, LANES, NT], F32)
        rstd = sb("rstd", [128, LANES, NT], F32)
        gmax = sb("gmax", [128, LANES, 2, NT], F32)
        geq = sb("geq", [128, LANES, NT, NE], F32)
        hot = sb("hot", [128, LANES, NT, NE], F32)
        rank = sb("rank", [128, NT, NE], F32)
        ident = sb("ident", [128, 128], F32)
        ident_b = sb("ident_b", [128, 128], BF16)
        mask_b = sb("mask_b", [128, TT], BF16)
        ones_pv = sb("ones_pv", [128, 3, 32], F32)
        vec = sb("vec", [128, 32], F32)
        lnb_b = sb("lnb_b", [128, 2, KT, TT], F32)
        row = sb("row", [128, 7, D], F32)
        bias_qk = sb("bias_qk", [128, 2, 4], F32)
        bias_f1 = sb("bias_f1", [64, 2], F32)
        stage = [pt[:].rearrange("p a b c -> p (a b c)")[:, 2048 * s:2048 * s + 2048] for s in range(2)]

        ps_g = [bank(f"ps_g{i}") for i in range(2)]
        ps_s = [bank(f"ps_s{i}") for i in range(2)]
        ps_t = [bank(f"ps_t{i}") for i in range(2)]
        ps_o, ps_d = bank("ps_o"), bank("ps_d")

        V_B1, V_G1, V_H1, V_G2, V_H2, V_BQ, V_F1 = 0, 4, 8, 12, 16, 20, 28
        R_B2, R_BO, R_F2, R_BV = 0, 1, 3, 5

        def v_view(l):
            return hv[l][0:TT].rearrange("p (k r a s d) -> p k r a s d", k=NT, r=2, s=2, d=16)

        def wslice(t, name, kt, lo, hi):
            at, _, n, rows = WCOL[name]
            return t[0:rows, at + kt * n + lo:at + kt * n + hi]

        c = {x: Count() for x in OWNER}
        g_use, rt_use = {}, {}
        g_reader, rt_user = [], []
        unit_slot, units = {}, []
        for spot, step in enumerate(ORDER):
            st, l = step[0], step[1]

            def add(name, key, n=1):
                c[name].add(key, n, spot, step)

            def use_bank(k, by, key):
                g_use[step, k] = len(g_reader)
                g_reader.append((by, key))
                add("g_full", (step, k))

            def split_rt():
                rt_use[step] = len(rt_user)
                rt_user.append(step)
                for x in ("r_done", "r_hi", "r_lo"):
                    add(x, step)

            if st == "xload":
                add(f"x_in{l}", step, 16)
            if st == "xin":
                add("x_hi", step)
                add("x_lo", step)
            if st in ("up", "f1"):
                use_bank(0, "r_done", step)
                split_rt()
            if st == "lnt" or st == "qkv" and step[3] < 4:
                for k in range(KT if st == "lnt" else 1):
                    use_bank(k, "lo", (step, k))
                    add("hi", (step, k))
                    add("lo", (step, k))
            if st == "qkv" and step[3] == 3 and step[2] == FIN:
                add("v_zero", step, 2)
            if st == "qkv" and step[3] >= 4:
                by = "vf_done" if step[2] == FIN else "v_done"
                use_bank(0, by, step)
                add(by, step, 2 if step[2] == FIN else 1)
            if st == "spill":
                add(f"scr{l}", step, 32)
            if st in ("down", "wo", "f2"):
                use_bank(0, "x_done", step)
                add("x_done", step)
            if st == "moe":
                use_bank(0, "x_done", (step, 1))
                add("x_done", (step, 0))
                add("x_done", (step, 1))
            if st == "out":
                add(f"out{l}", step, 16)
            if st == "fill":
                u = step[1]
                unit_slot[u] = len(units) % 2
                units.append(u)
                add(f"st_in{unit_slot[u]}", u, 16 * (8 if u[1] == FIN else 6))
            if st == "S":
                for i in range(NT):
                    add("s_full", (*step[1:], i))
                    add("s_max", (*step[1:], i))
            if st == "nm":
                use_bank(0, "nm_row", step[1])
                add("nm_row", step[1])
            if st == "T":
                for j in range(4):
                    add("t_full", (*step[1:], j))
                    add("exp", (*step[1:], j))
                if step[1][1] == FIN:
                    add("causal", step[1:])
            if st == "pv":
                add("o_full", step[1:])
            if st == "norm":
                add("den", (step, 0))
                add("den", (step, 1))
                split_rt()
            if st == "lnv":
                add("ln_st", step, NT)
                add("ln_mv", step, NT)
                add("ln_log", step)
                add("ln_rstd", step)
                add("h_done", step, NT)
                if step[2:] == (FIN, 1):
                    add("z_done", l)
                elif step[2] != FIN:
                    add("x_bias", step)
            if st == "gate":
                use_bank(0, "gate", (step, 2))
                for k in (1, 2, 3, 4):
                    add("gate", (step, k))
                add("hot", step)
        assert len(g_reader) % 2 == len(rt_user) % 2 == len(units) % 2 == 0
        norms = [i for i in ORDER if i[0] == "norm"]
        s_uses, t_uses = list(c["s_max"].after), list(c["exp"].after)
        sems = {x: sem(x) for x in c}
        zeroed, zeroed_p, loaded0, loaded1, split_hi, split_lo, consts, ident_ok, alibi_ok, alibi_in, small_in, bias_mm, bias_ok, ready = (sem(x) for x in (
            "zeroed", "zeroed_p", "loaded0", "loaded1", "split_hi", "split_lo", "consts", "ident_ok", "alibi_ok", "alibi_in", "small_in", "bias_mm", "bias_ok", "ready"))
        here = [0]

        def waits(eng, turn):
            def after(name, key):
                behind = 1 if c[name].spot[key] > here[0] else 0
                eng.wait_ge(sems[name], turn * c[name].total + (c[name].total * (1 - behind) + c[name].after[key]))

            def ago(name, keys, key, back):
                after(name, keys[keys.index(key) - back])

            def bank_free(u):
                after(*g_reader[u - 2])
            return after, ago, bank_free

        held = sem("held")

        def credit(eng, name):
            for x in OWNER:
                if OWNER[x] == name and not x.startswith("x_in"):
                    eng.sem_inc(sems[x], c[x].total)

        def steps(eng, name, turn):
            owed, level = {}, {x: c[x].total * (turn + 1) for x in OWNER} if isinstance(turn, int) else {}

            def settle(step):
                if owed and name != "sp":
                    eng.drain()
                for x, n in owed.items():
                    if name == "sp":
                        eng.wait_ge(sems[x], level[x])
                    eng.sem_inc(sems[x], n)
                    level[x] += n
                owed.clear()
                for x in level:
                    level[x] += c[x].by_step.get(step, 0)

            for here[0], step in enumerate(ORDER):
                late = step in LATE
                if isinstance(turn, int) and (turn == 0) == late:
                    for x in OWNER:
                        if OWNER[x] == name and step in c[x].by_step:
                            owed[x] = owed.get(x, 0) + c[x].by_step[step]
                    continue
                settle(step)
                yield step
            settle(None)

        def turns(eng, body):
            body(0)
            with eng.Fori(1, TURNS) as turn:
                body(turn)
            body(TURNS)

        chunks = [("W1", 0, KT, 0, DFF, None), ("W2", 0, MT, 0, D, None)]
        for n in (0, 1):
            chunks += [(f"qkv{n}", 0, KT, 0, 3 * D, V_G1 + 2 * n), (f"o{n}", 0, KT, 0, D, None),
                       (f"f1{n}", 0, KT, 0, FH, V_G2 + 2 * n), (f"f2{n}", 0, 1, 0, D, None)]
        chunks += [("qkv2", 0, KT, 0, 3 * D, None), ("o2", 0, KT, 0, D, None),
                   ("gate", 0, KT, 0, NE, None)]
        chunks += [("exp", kt, 1, 0, NE * D, None) for kt in range(KT)]

        loaded = [loaded0, loaded1]

        def staged(k):
            name, kt0, kts, lo, hi, _ = chunks[k]
            rows = WCOL[name][3]
            return stage[k % 2][0:rows, 0:kts * (hi - lo)].rearrange("p (k n) -> p k n", k=kts)

        def parts(k):
            name, kt0, kts, lo, hi, g = chunks[k]
            at, _, n, rows = WCOL[name]
            v = [t[0:rows, at + kt0 * n:at + (kt0 + kts) * n].rearrange("p (k n) -> p k n", k=kts)
                 for t in (w_hi, w_lo)]
            if g is None:
                yield staged(k), v[0], v[1], None
            else:
                for kt in range(kts):
                    yield staged(k)[:, kt, :], v[0][:, kt, :], v[1][:, kt, :], vec[0:rows, g + kt:g + kt + 1]

        nparts = [len(list(parts(k))) for k in range(len(chunks))]
        upto = [sum(nparts[:k + 1]) for k in range(len(chunks))]
        biased = [k for k, ch in enumerate(chunks) if ch[5] is not None]

        block = ctx.enter_context(nc.Block())

        @block.sync
        def _(sp):
            sp.dma_start(vec[:], small["vec"]).then_inc(small_in, 16)
            sp.dma_start(row[0:TT], small["row"].partition_broadcast(TT)).then_inc(small_in, 16)
            sp.dma_start(rank[:], small["rank"].partition_broadcast(128)).then_inc(small_in, 16)
            sp.dma_start(rt[0][0:64, :], alibi_q).then_inc(small_in, 16)
            sp.dma_start(rt[1][0:MROW - 48, :], alibi_k).then_inc(small_in, 16)
            for k in range(len(chunks)):
                name, kt0, kts, lo, hi, _ = chunks[k]
                if k >= 2:
                    sp.wait_ge(split_lo, upto[k - 2])
                    nb = len([b for b in biased if b <= k - 2])
                    if nb:
                        sp.wait_ge(bias_mm, nb)
                sp.dma_start(staged(k), w[name][:, kt0:kt0 + kts, :]).then_inc(loaded[k % 2], 16)
            sp.wait_ge(alibi_ok, 2)
            sp.dma_start(ali_q, b_hi[0][0:64, 0, 0:T].bitcast(F32)).then_inc(alibi_in, 16)
            sp.dma_start(ali_k, b_hi[0][0:MROW - 48, 1, 0:T].bitcast(F32)).then_inc(alibi_in, 16)
            sp.wait_ge(alibi_in, 32)
            sp.sem_inc(ready, 1)
            credit(sp, "sp")
            for l in range(LANES):
                sp.dma_start(hv[l][:, 3 * D:3 * D + KT * T], xT[l]).then_inc(sems[f"x_in{l}"], 16)
            sp.wait_ge(ready, 5)

            def body(turn):
                after, ago, bank_free = waits(sp, turn)
                seq = {}
                for l in range(LANES):
                    for k, ahead in (("xload", 1), ("out", 0)):
                        s = turn * LANES + (LANES * (ahead - ((k, l) in LATE)) + l)
                        seq[k, l] = s if isinstance(turn, int) else sp.snap(s)
                for step in steps(sp, "sp", turn):
                    kind, l = step[0], step[1]
                    if kind == "xload":
                        after("o_full", ((l, FIN, GROUPS[FIN] - 1), NT - 1))
                        sp.dma_start(hv[l][:, 3 * D:3 * D + KT * T], xT[bass.ds(seq[step], 1)].rearrange(
                            "o p n -> (o p) n")).then_inc(sems[f"x_in{l}"], 16)
                    if kind == "spill":
                        n = step[2]
                        after("lo", (("qkv", l, n, 3), 0))
                        for x, part in enumerate((b_hi, b_lo)):
                            sp.dma_start(scr[l][x][:, :, 0:T], part[l][:, :, 0:T].bitcast(F32)
                                         ).then_inc(sems[f"scr{l}"], 16)
                    if kind == "fill":
                        u = l, n, g = step[1]
                        s = unit_slot[u]
                        if g == 0:
                            after(f"scr{l}", ("spill", l, n))
                            sp.sem_inc(held, 1)
                        p = units[units.index(u) - 2]
                        after("exp", (p, NT - 1, 3))
                        hd = HD[n]
                        m, way = (g, 0) if n != FIN else (g // 2, g % 2)
                        for r, (qx, kx) in enumerate(((0, 0), (1, 0), (0, 1))):
                            for st, x, mt in ((q_st, qx, m), (k_st, kx, 2 + m)):
                                sp.dma_start(st[s][hd * r:hd * r + hd, :, 0:T].bitcast(F32),
                                             scr[l][x][:, mt, 0:T].rearrange("(j w p) t -> w p j t", j=4, p=hd)[way]
                                             ).then_inc(sems[f"st_in{s}"], 16)
                        if n == FIN:
                            sp.dma_start(q_st[s][48:52, :, 0:T].bitcast(F32),
                                         ali_q.rearrange("(g j r) t -> g r j t", g=4, r=4)[g]
                                         ).then_inc(sems[f"st_in{s}"], 16)
                            sp.dma_start(k_st[s][48:MROW, :, 0:T].bitcast(F32),
                                         ali_k[:, None, :].to_broadcast([MROW - 48, 4, T])
                                         ).then_inc(sems[f"st_in{s}"], 16)
                    if kind == "out":
                        after("x_done", (("moe", l, NT - 1, NE // 2 - 1), 1))
                        sp.dma_start(out[bass.ds(seq[step], 1)].rearrange("o (i p) d -> (o p) i d", p=TT),
                                     xres[l][0:TT]).then_inc(sems[f"out{l}"], 16)

            turns(sp, body)
            for l in range(LANES):
                sp.wait_ge(sems[f"out{l}"], 16 * (TURNS + 2))
                sp.wait_ge(sems[f"x_in{l}"], 16 * (TURNS + 2))

        @block.tensor
        def _(pe):
            pe.wait_ge(ident_ok, 3)
            pe.wait_ge(consts, NCONST)
            for b, k in enumerate(biased):
                n, f1 = b // 2, b % 2
                pe.wait_ge(loaded[k % 2], 16 * (k // 2 + 1))
                if b:
                    pe.wait_ge(bias_ok, [2, 3, 5, 6][b - 1])
                src, mm_n = staged(k), FH if f1 else 128
                for m in range(1 if f1 else 4):
                    for kt in range(KT):
                        at = (V_H2 if f1 else V_H1) + 2 * n + kt
                        mm = pe.matmul(ps_g[0][0:mm_n, m:m + 1], src[:, kt, 128 * m:128 * m + mm_n],
                                       vec[:, at:at + 1], start=kt == 0, stop=kt == KT - 1)
                if not f1:
                    for kt in range(KT):
                        mm = pe.matmul(ps_g[1][0:TT, 0:D], lnb_b[:, n, kt, :], src[:, kt, 2 * D:3 * D],
                                       start=kt == 0, stop=kt == KT - 1)
                mm.then_inc(bias_mm, 1)
            credit(pe, "pe")
            pe.drain().then_inc(ready, 1)
            pe.wait_ge(ready, 5)

            def passes(dst, terms, done=None):
                k = 0
                for st, mv_ in terms:
                    for a, b in ((1, 0), (0, 1), (0, 0)):
                        mm = pe.matmul(dst, st[a], mv_[b], start=k == 0, stop=k == 3 * len(terms) - 1)
                        k += 1
                if done is not None:
                    mm.then_inc(done, 1)

            def wpair(name, kt, lo, hi):
                return wslice(w_hi, name, kt, lo, hi), wslice(w_lo, name, kt, lo, hi)

            def bypart(t, l, kt, lo, hi, rows=128):
                return t[0][l][0:rows, kt, lo:hi], t[1][l][0:rows, kt, lo:hi]

            def body(turn):
                after, ago, bank_free = waits(pe, turn)
                AB, BB = (a_hi, a_lo), (b_hi, b_lo)

                for step in steps(pe, "pe", turn):
                    kind, l = step[0], step[1]
                    if (step, 0) in g_use and kind != "nm":
                        u = g_use[step, 0]
                        bank = ps_g[u % 2]
                    if kind == "up":
                        m = step[2]
                        if m == 0:
                            after("x_lo", ("xin", l))
                        bank_free(u)
                        passes(bank[:, 0:TP], [(wpair("W1", kt, 128 * m, 128 * m + 128),
                                                bypart(AB, l, kt, 0, TP)) for kt in range(KT)], sems["g_full"])
                    if kind == "down":
                        i = step[2]
                        if i == 0:
                            after("r_lo", ("up", l, MT - 1))
                        bank_free(u)
                        passes(bank[0:TT, 0:D], [(bypart(BB, l, kt, TT * i, TT * i + TT), wpair("W2", kt, 0, D))
                                                 for kt in range(MT)], sems["g_full"])
                    if kind == "lnt":
                        after("h_done", ("lnv", *step[1:]))
                        for kt in range(KT):
                            u = g_use[step, kt]
                            bank_free(u)
                            for i in range(NT):
                                mm = pe.transpose(ps_g[u % 2][:, TT * i:TT * i + TT],
                                                  hv[l][0:TT, D * i + 128 * kt:D * i + 128 * kt + 128],
                                                  ident[0:TT, 0:TT])
                            mm.then_inc(sems["g_full"], 1)
                    if kind == "qkv":
                        n, m = step[2:]
                        if m == 0:
                            after("lo", (("lnt", l, n, 0), KT - 1))
                        bank_free(u)
                        if m < 4:
                            passes(bank[:, 0:TP], [(wpair(f"qkv{n}", kt, 128 * m, 128 * m + 128),
                                                    bypart(AB, l, kt, 0, TP)) for kt in range(KT)], sems["g_full"])
                        else:
                            i = m - 4
                            passes(bank[0:TT, 0:D], [(bypart(AB, l, kt, TT * i, TT * i + TT),
                                                      wpair(f"qkv{n}", kt, 2 * D, 3 * D)) for kt in range(KT)],
                                   sems["g_full"])
                    if kind == "S":
                        su, j = step[1:]
                        s, n = unit_slot[su], su[1]
                        if j == 0:
                            after(f"st_in{s}", su)
                        for i in range(NT):
                            b = ps_s[s_uses.index((su, j, i)) % 2]
                            ago("s_max", s_uses, (su, j, i), 2)
                            cols = TP if n != FIN or i == NT - 1 else (TT * (i + 1) + 1) // 2 * 2
                            mm = pe.matmul(b[0:TT, 0:cols], q_st[s][0:MROW, j, TT * i:TT * i + TT],
                                           k_st[s][0:MROW, j, 0:cols], start=True, stop=n != FIN)
                            if n == FIN:
                                mm = pe.matmul(b[0:TT, TT * i:TT * i + TT], ident_b[0:TT, 0:TT],
                                               mask_b[0:TT, :], start=False, stop=True)
                            mm.then_inc(sems["s_full"], 1)
                    if kind == "nm":
                        un = step[1]
                        u = g_use[step, 0]
                        after("s_max", (un, 3, NT - 1))
                        bank_free(u)
                        for i in range(NT):
                            mm = pe.matmul(ps_g[u % 2][MROW:MROW + 4, TT * i:TT * i + TT],
                                           nmx[unit_slot[un]][0:TT, 4 * i:4 * i + 4], ident[0:TT, 0:TT],
                                           start=True, stop=True)
                        mm.then_inc(sems["g_full"], 1)
                    if kind == "T":
                        tu, kt = step[1:]
                        s, n = unit_slot[tu], tu[1]
                        if kt == 0:
                            after("nm_row", tu)
                        for j in range(4):
                            b = ps_t[t_uses.index((tu, kt, j)) % 2]
                            ago("exp", t_uses, (tu, kt, j), 2)
                            q0 = TT * kt // 2 * 2 if n == FIN else 0
                            pe.matmul(b[0:TT, 0:TP - q0], k_st[s][0:MROW + 4, j, TT * kt:TT * kt + TT],
                                      q_st[s][0:MROW + 4, j, q0:TP], start=True, stop=True
                                      ).then_inc(sems["t_full"], 1)
                    if kind == "pv":
                        un, kt = step[1:]
                        l, n, g = un
                        if n == FIN:
                            after("causal", (un, kt))
                        else:
                            after("exp", (un, kt, 3))
                        if g == 0 and kt == 0:
                            after("vf_done" if n == FIN else "v_done", ("qkv", l, n, 3 + NT))
                            if n == FIN:
                                after("v_zero", ("qkv", l, n, 3))
                        first, final = (g % 2 == 0, g % 2 == 1) if n == FIN else (True, True)
                        if first and kt == 0:
                            norm = ("norm", (l, n, g + (n == FIN)))
                            ago("r_done", norms, norm, 1)
                        q0 = TT * kt if n == FIN else 0
                        for j in range(4):
                            if n == FIN:
                                at = 512 * kt + 256 * (g % 2) + 128 * (g // 2) + 32 * j
                            else:
                                at = 3 * D + D * kt + 128 * g + 32 * j
                            pe.matmul(ps_o[32 * j:32 * j + 32, q0:T], hv[l][0:TT, at:at + 32],
                                      pt[0:TT, j, kt, q0:T], start=first and kt == 0,
                                      stop=final and kt == NT - 1)
                        for j in range(4):
                            mm = pe.matmul(ps_d[32 * j:32 * j + 32, q0:T],
                                           ones_pv[0:TT, 1 + g % 2 if n == FIN else 0, :],
                                           pt[0:TT, j, kt, q0:T], start=first and kt == 0,
                                           stop=final and kt == NT - 1)
                        mm.then_inc(sems["o_full"], 1)
                    if kind == "wo":
                        n, i = step[2:]
                        if i == 0:
                            after("r_lo", ("norm", (l, n, GROUPS[n] - 1)))
                        bank_free(u)
                        passes(bank[0:TT, 0:D], [(bypart(AB, l, kt, TT * i, TT * i + TT),
                                                  wpair(f"o{n}", kt, 0, D)) for kt in range(KT)], sems["g_full"])
                    if kind == "f1":
                        n = step[2]
                        after("lo", (("lnt", l, n, 1), KT - 1))
                        bank_free(u)
                        passes(bank[0:FH, 0:TP], [(wpair(f"f1{n}", kt, 0, FH), bypart(AB, l, kt, 0, TP))
                                                  for kt in range(KT)], sems["g_full"])
                    if kind == "f2":
                        n, i = step[2:]
                        if i == 0:
                            after("r_lo", ("f1", l, n))
                        bank_free(u)
                        passes(bank[0:TT, 0:D], [(bypart(BB, l, 0, TT * i, TT * i + TT, FH),
                                                  wpair(f"f2{n}", 0, 0, D))], sems["g_full"])
                    if kind == "gate":
                        after("lo", (("lnt", l, FIN, 1), KT - 1))
                        bank_free(u)
                        for i in range(NT):
                            passes(bank[0:TT, NE * i:NE * i + NE],
                                   [(bypart(AB, l, kt, TT * i, TT * i + TT), wpair("gate", kt, 0, NE))
                                    for kt in range(KT)], sems["g_full"] if i == NT - 1 else None)
                    if kind == "moe":
                        i, e = step[2:]
                        bank_free(u)
                        passes(bank[0:TT, :], [(bypart(AB, l, kt, TT * i, TT * i + TT),
                                                wpair("exp", kt, 2 * e * D, 2 * (e + 1) * D))
                                               for kt in range(KT)], sems["g_full"])

            turns(pe, body)

        @block.scalar
        def _(act):
            act.add_instruction(mybir.InstLoadActFuncSet(name=nc.get_next_instruction_name(),
                                                         act_func_set_id=EXP_LN_SET, ins=[], outs=[]))
            act.wait_ge(small_in, 16 * 5)
            act.copy(b_hi[0][0:64, 0, 0:T], rt[0][0:64, 0:T]).then_inc(alibi_ok, 1)
            act.copy(b_hi[0][0:MROW - 48, 1, 0:T], rt[1][0:MROW - 48, 0:T]).then_inc(alibi_ok, 1)
            for k in range(len(chunks)):
                act.wait_ge(loaded[k % 2], 16 * (k // 2 + 1))
                for src, hi, _, g in parts(k):
                    if g is None:
                        act.copy(hi, src).then_inc(split_hi, 1)
                    else:
                        act.activation(hi, src, ACT.Copy, scale=g).then_inc(split_hi, 1)
            credit(act, "act")
            act.drain().then_inc(ready, 1)
            act.wait_ge(ready, 5)

            def body(turn):
                after, ago, bank_free = waits(act, turn)
                for step in steps(act, "act", turn):
                    kind, l = step[0], step[1]
                    if kind == "xin":
                        after(f"x_in{l}", ("xload", l))
                        after("g_full", (("moe", l, NT - 1, NE // 2 - 1), 0))
                        act.copy(a_hi[l][:, :, 0:T], hv[l][:, 3 * D:3 * D + KT * T].rearrange(
                            "p (k t) -> p k t", k=KT)).then_inc(sems["x_hi"], 1)
                    if kind == "norm":
                        after("o_full", (step[1], NT - 1))
                        act.activation(lden[:], ps_d[:, 0:T], ACT.Ln).then_inc(sems["den"], 1)
                        after("den", (step, 0))
                        ago("r_done", norms, step, 1)
                        act.activation(rden[:], lden[:], ACT.Exp, scale=-1.0).then_inc(sems["den"], 1)
                    if step in rt_use:
                        if kind == "norm":
                            l, n, g = step[1]
                            dst = a_hi[l][:, g // 2 if n == FIN else g, 0:T]
                        else:
                            dst = b_hi[l][:, step[2], 0:T] if kind == "up" else b_hi[l][0:FH, 0, 0:T]
                        after("r_done", step)
                        act.copy(dst, rt[rt_use[step] % 2][0:dst.shape[0], 0:T]).then_inc(sems["r_hi"], 1)
                    if kind == "lnt" or kind == "qkv" and step[3] < 4:
                        for k in range(KT if kind == "lnt" else 1):
                            after("g_full", (step, k))
                            src = ps_g[g_use[step, k] % 2][:, 0:T]
                            if kind == "lnt":
                                act.copy(a_hi[l][:, k, 0:T], src).then_inc(sems["hi"], 1)
                            elif step[2] == FIN:
                                act.copy(b_hi[l][:, step[3], 0:T], src).then_inc(sems["hi"], 1)
                            else:
                                m = step[3]
                                act.activation(b_hi[l][:, m, 0:T], src, ACT.Identity,
                                               bias=bias_qk[:, step[2], m:m + 1]).then_inc(sems["hi"], 1)
                    if kind == "qkv" and step[2] == FIN and step[3] >= 4:
                        after("g_full", (step, 0))
                        src = ps_g[g_use[step, 0] % 2][0:TT, 0:D].rearrange("p (a s d) -> p a s d", s=2, d=16)
                        for r in range(2):
                            act.copy(v_view(l)[:, step[3] - 4, r, :, r, :], src[:, :, r, :]).then_inc(sems["vf_done"], 1)
                    if kind == "nm":
                        un = step[1]
                        after("g_full", (step, 0))
                        act.copy(q_st[unit_slot[un]][MROW:MROW + 4, :, 0:T],
                                 ps_g[g_use[step, 0] % 2][MROW:MROW + 4, None, 0:T].to_broadcast([4, 4, T])
                                 ).then_inc(sems["nm_row"], 1)
                    if kind == "T":
                        un, kt = step[1:]
                        n = un[1]
                        for j in range(4):
                            after("t_full", (un, kt, j))
                            if j == 0:
                                ago("o_full", [(x, kt) for x in units], (un, kt), 1)
                            q0 = TT * kt if n == FIN else 0
                            b = ps_t[t_uses.index((un, kt, j)) % 2]
                            act.activation(pt[0:TT, j, kt, q0:T], b[0:TT, q0 % 2:q0 % 2 + T - q0],
                                           ACT.Exp, scale=SCALE[n]).then_inc(sems["exp"], 1)
                    if kind == "lnv":
                        after("ln_mv", step)
                        act.activation(lnv_t[0:TT, l, :], mv[0:TT, l, :, 1], ACT.Ln,
                                       bias=EPS_FIN if step[2] == FIN else EPS_TOK).then_inc(sems["ln_log"], 1)
                        after("ln_log", step)
                        act.activation(rstd[0:TT, l, :], lnv_t[0:TT, l, :], ACT.Exp,
                                       scale=-0.5).then_inc(sems["ln_rstd"], 1)

            turns(act, body)

        @block.vector
        def _(dve):
            for l in range(LANES):
                for t in (a_hi, a_lo, b_hi, b_lo):
                    dve.memset(t[l][:, :, T:TP].bitcast(F32), 0.0).then_inc(consts, 1)
            for s in range(2):
                dve.memset(q_st[s][:].bitcast(F32), 0.0).then_inc(consts, 1)
                dve.memset(k_st[s][:].bitcast(F32), 0.0).then_inc(zeroed, 1)
            dve.wait_ge(zeroed, 2)
            dve.wait_ge(ident_ok, 3)
            for s in range(2):
                for j in range(4):
                    dve.tensor_copy(k_st[s][MROW:MROW + 4, j, :], ident[MROW:MROW + 4, MROW + j:MROW + j + 1
                                                                        ].to_broadcast([4, TP])).then_inc(consts, 1)
            dve.memset(ones_pv[:], 0.0).then_inc(zeroed, 1)
            dve.wait_ge(zeroed, 3)
            dve.memset(ones_pv[:, 0, :], 1.0).then_inc(consts, 1)
            for r in range(2):
                dve.memset(ones_pv[:, 1 + r, 16 * r:16 * r + 16], 1.0).then_inc(consts, 1)
            dve.wait_ge(small_in, 16 * 5)
            for n in range(2):
                for kt in range(KT):
                    at = V_H1 + 2 * n + kt
                    if n == kt == 0:
                        dve.memset(lnb_b[:], 0.0).then_inc(zeroed, 1)
                        dve.wait_ge(zeroed, 4)
                    dve.tensor_scalar(lnb_b[:, n, kt, :], lnb_b[:, n, kt, :], vec[:, at:at + 1], None, ALU.add
                                      ).then_inc(consts, 1)
            done = 0
            for k in range(len(chunks)):
                for src, hi, lo, g in parts(k):
                    done += 1
                    dve.wait_ge(split_hi, done)
                    if g is None:
                        dve.tensor_tensor(lo, src, hi.bitcast(F32), ALU.subtract).then_inc(split_lo, 1)
                    else:
                        dve.scalar_tensor_tensor(out=lo, in0=src, scalar=g, in1=hi.bitcast(F32),
                                                 op0=ALU.mult, op1=ALU.subtract).then_inc(split_lo, 1)
                if k in biased:
                    b = biased.index(k)
                    n, f1 = b // 2, b % 2
                    dve.wait_ge(bias_mm, b + 1)
                    if f1:
                        dve.tensor_tensor(bias_f1[:, n:n + 1], ps_g[0][0:FH, 0:1], vec[0:FH, V_F1 + n:V_F1 + n + 1],
                                          ALU.add).then_inc(bias_ok, 1)
                    else:
                        dve.tensor_tensor(bias_qk[:, n, :], ps_g[0][:, 0:4], vec[:, V_BQ + 4 * n:V_BQ + 4 * n + 4],
                                          ALU.add).then_inc(bias_ok, 1)
                        dve.tensor_tensor(row[0:TT, R_BV + n, :], ps_g[1][0:TT, 0:D], row[0:TT, R_BV + n, :],
                                          ALU.add).then_inc(bias_ok, 1)
            credit(dve, "dve")
            dve.drain().then_inc(ready, 1)
            dve.wait_ge(ready, 5)

            def body(turn):
                after, ago, bank_free = waits(dve, turn)

                def gbank(step, k=0):
                    after("g_full", (step, k))
                    return ps_g[g_use[step, k] % 2]

                for step in steps(dve, "dve", turn):
                    kind, l = step[0], step[1]
                    if step in rt_use:
                        k = rt_use[step]
                        after("r_lo", rt_user[k - 2])
                        if kind == "norm":
                            after("den", (step, 1))
                            dve.tensor_tensor(rt[k % 2][:, 0:T], ps_o[:, 0:T], rden[:], ALU.mult
                                              ).then_inc(sems["r_done"], 1)
                        elif kind == "up":
                            m = step[2]
                            dve.tensor_scalar(rt[k % 2][:, 0:T], gbank(step)[:, 0:T],
                                              vec[:, V_B1 + m:V_B1 + m + 1], 0.0, ALU.add, ALU.max
                                              ).then_inc(sems["r_done"], 1)
                        else:
                            dve.tensor_scalar(rt[k % 2][0:FH, 0:T], gbank(step)[0:FH, 0:T],
                                              bias_f1[:, step[2]:step[2] + 1], 0.0, ALU.add, ALU.max
                                              ).then_inc(sems["r_done"], 1)
                    if kind == "down":
                        i = step[2]
                        if i == 0:
                            after(f"out{l}", ("out", l))
                        dve.tensor_tensor(xres[l][0:TT, i, :], gbank(step)[0:TT, 0:D], row[0:TT, R_B2, :],
                                          ALU.add).then_inc(sems["x_done"], 1)
                    if kind in ("wo", "f2"):
                        n, i = step[2:]
                        if n != FIN and i == 0:
                            after("x_bias", ("lnv", l, n, int(kind == "f2")))
                        dve.tensor_tensor(xres[l][0:TT, i, :], gbank(step)[0:TT, 0:D], xres[l][0:TT, i, :],
                                          ALU.add).then_inc(sems["x_done"], 1)
                    if kind == "lnv":
                        _, _, n, k2 = step
                        src = ("wo", l, n) if k2 else ("down", l) if n == 0 else ("f2", l, n - 1)
                        after("x_done", (*src, NT - 1))
                        for i in range(NT):
                            dve.bn_stats(stats[0:TT, l, i, :], xres[l][0:TT, i, :]).then_inc(sems["ln_st"], 1)
                        after("ln_st", step)
                        dve.sem_inc(held, 1)
                        for i in range(NT):
                            dve.bn_aggr(mv[0:TT, l, i, :], stats[0:TT, l, i, :]).then_inc(sems["ln_mv"], 1)
                        after("ln_rstd", step)
                        for i in range(NT):
                            dve.tensor_scalar(hv[l][0:TT, D * i:D * i + D], xres[l][0:TT, i, :],
                                              mv[0:TT, l, i, 0:1], rstd[0:TT, l, i:i + 1],
                                              ALU.subtract, ALU.mult).then_inc(sems["h_done"], 1)
                    if kind == "lnt" or kind == "qkv" and step[3] < 4:
                        for k in range(KT if kind == "lnt" else 1):
                            after("hi", (step, k))
                            src = ps_g[g_use[step, k] % 2][:, 0:T]
                            thi, tlo = (a_hi, a_lo) if kind == "lnt" else (b_hi, b_lo)
                            m = k if kind == "lnt" else step[3]
                            if kind == "qkv" and step[2] != FIN:
                                dve.scalar_tensor_tensor(out=tlo[l][:, m, 0:T], in0=src,
                                                         scalar=bias_qk[:, step[2], m:m + 1],
                                                         in1=thi[l][:, m, 0:T].bitcast(F32), op0=ALU.add,
                                                         op1=ALU.subtract).then_inc(sems["lo"], 1)
                            else:
                                dve.tensor_tensor(tlo[l][:, m, 0:T], src, thi[l][:, m, 0:T].bitcast(F32),
                                                  ALU.subtract).then_inc(sems["lo"], 1)
                    if kind == "qkv" and step[2] != FIN and step[3] >= 4:
                        i = step[3] - 4
                        dve.tensor_tensor(hv[l][0:TT, (3 + i) * D:(4 + i) * D], gbank(step)[0:TT, 0:D],
                                          row[0:TT, R_BV + step[2], :], ALU.add).then_inc(sems["v_done"], 1)
                    if kind == "S":
                        u, j = step[1:]
                        s, n = unit_slot[u], u[1]
                        for i in range(NT):
                            if j == i == 0:
                                ago("nm_row", units, u, 2)
                            after("s_full", (u, j, i))
                            w = TT * (i + 1) if n == FIN else T
                            dve.tensor_reduce(nmx[s][0:TT, 4 * i + j:4 * i + j + 1],
                                              ps_s[s_uses.index((u, j, i)) % 2][0:TT, 0:w],
                                              AX.X, ALU.max, negate=True).then_inc(sems["s_max"], 1)
                    if kind == "gate":
                        def wide(t):
                            return t[:, :, None].to_broadcast([TT, NT, NE])
                        sc = gbank(step)[0:TT, 0:NT * NE].rearrange("p (i e) -> p i e", i=NT)
                        dve.tensor_reduce(gmax[0:TT, l, 0, :], sc, AX.X, ALU.max).then_inc(sems["gate"], 1)
                        after("gate", (step, 1))
                        dve.tensor_tensor(geq[0:TT, l], sc, wide(gmax[0:TT, l, 0, :]), ALU.is_equal
                                          ).then_inc(sems["gate"], 1)
                        after("gate", (step, 2))
                        dve.tensor_tensor(hot[0:TT, l], geq[0:TT, l], rank[0:TT], ALU.mult).then_inc(sems["gate"], 1)
                        after("gate", (step, 3))
                        dve.tensor_reduce(gmax[0:TT, l, 1, :], hot[0:TT, l], AX.X, ALU.max).then_inc(sems["gate"], 1)
                        after("gate", (step, 4))
                        dve.tensor_tensor(hot[0:TT, l], hot[0:TT, l], wide(gmax[0:TT, l, 1, :]), ALU.is_equal
                                          ).then_inc(sems["hot"], 1)
                    if kind == "moe":
                        i, e = step[2:]
                        if i == e == 0:
                            after("z_done", l)
                            after("hot", ("gate", l))
                        bk = gbank(step)
                        for x in range(2):
                            if e or x:
                                after("x_done", (step, 0) if x else ((*step[:3], e - 1), 1))
                            ex = 2 * e + x
                            dve.scalar_tensor_tensor(out=xres[l][0:TT, i, :], in0=bk[0:TT, D * x:D * x + D],
                                                     scalar=hot[0:TT, l, i, ex:ex + 1], in1=xres[l][0:TT, i, :],
                                                     op0=ALU.mult, op1=ALU.add).then_inc(sems["x_done"], 1)

            turns(dve, body)

        @block.gpsimd
        def _(pool):
            for t in (ident, ident_b, mask_b):
                pool.memset(t[:], 0.0).then_inc(zeroed_p, 1)
            pool.wait_ge(zeroed_p, 3)
            for t in (ident, ident_b):
                pool.affine_select(out=t[:], in_=t[:], compare_op=ALU.not_equal, fill=1.0, base=0,
                                   pattern=[[-1, 128]], channel_multiplier=1).then_inc(ident_ok, 1)
            pool.affine_select(out=mask_b[:], in_=mask_b[:], compare_op=ALU.is_ge, fill=MASKED, base=0,
                               pattern=[[-1, TT]], channel_multiplier=1).then_inc(ident_ok, 1)
            credit(pool, "pool")
            pool.drain().then_inc(ready, 1)
            pool.wait_ge(ready, 5)

            def body(turn):
                after, ago, bank_free = waits(pool, turn)
                for step in steps(pool, "pool", turn):
                    kind, l = step[0], step[1]
                    if kind == "xin":
                        after("x_hi", step)
                        pool.tensor_tensor(a_lo[l][:, :, 0:T], hv[l][:, 3 * D:3 * D + KT * T].rearrange(
                            "p (k t) -> p k t", k=KT), a_hi[l][:, :, 0:T].bitcast(F32), ALU.subtract
                            ).then_inc(sems["x_lo"], 1)
                    if step in rt_use:
                        if kind == "norm":
                            l, n, g = step[1]
                            k = g // 2 if n == FIN else g
                            hi, lo = a_hi[l][:, k, 0:T], a_lo[l][:, k, 0:T]
                        else:
                            rows, k = (128, step[2]) if kind == "up" else (FH, 0)
                            hi, lo = b_hi[l][0:rows, k, 0:T], b_lo[l][0:rows, k, 0:T]
                        after("r_hi", step)
                        pool.tensor_tensor(lo, rt[rt_use[step] % 2][0:hi.shape[0], 0:T], hi.bitcast(F32),
                                           ALU.subtract).then_inc(sems["r_lo"], 1)
                    if kind == "lnv" and step[2:] != (FIN, 0):
                        _, _, n, k2 = step
                        after("h_done", step)
                        if n == FIN:
                            pool.tensor_tensor(xres[l][0:TT], xres[l][0:TT],
                                               hv[l][0:TT, 0:NT * D].rearrange("p (i d) -> p i d", i=NT), ALU.add
                                               ).then_inc(sems["z_done"], 1)
                        else:
                            at = (R_F2 if k2 else R_BO) + n
                            pool.tensor_tensor(xres[l][0:TT], xres[l][0:TT],
                                               row[0:TT, at:at + 1, :].to_broadcast([TT, NT, D]), ALU.add
                                               ).then_inc(sems["x_bias"], 1)
                    if kind == "qkv" and step[2] == FIN and step[3] == 3:
                        after("hi", (("lnt", l, FIN, 0), KT - 1))
                        pool.sem_inc(held, 1)
                        for r in range(2):
                            pool.memset(v_view(l)[:, :, r, :, 1 - r, :], 0.0).then_inc(sems["v_zero"], 1)
                    if kind == "T" and step[1][1] == FIN:
                        kt = step[2]
                        after("exp", (*step[1:], 3))
                        pool.sem_inc(held, 1)
                        pd = pt[0:TT, :, kt, TT * kt:TT * kt + TT]
                        pool.affine_select(out=pd, in_=pd, compare_op=ALU.is_ge, fill=0.0, base=0,
                                           pattern=[[0, 4], [1, TT]], channel_multiplier=-1
                                           ).then_inc(sems["causal"], 1)

            turns(pool, body)


def alibi_rows():
    def halves(x):
        x = np.float32(x)
        b = x.view(np.uint32)
        hi = ((b + np.uint32(0x7FF) + ((b >> 12) & 1)) & np.uint32(0xFFFFF000)).view(np.float32)
        return hi, np.float32(x - hi)

    pos = np.arange(TP, dtype=np.float32)
    q = np.zeros((64, TP), np.float32)
    for g in range(4):
        for j in range(4):
            h = 8 * (g // 2) + 2 * j + g % 2
            slope = np.float32(2.0) ** np.float32(-8.0 / 16 * (h + 1)) / np.float32(SCALE[FIN])
            at = 16 * g + 4 * j
            q[at], q[at + 1] = halves(slope)
            q[at + 2], q[at + 3] = halves(-(np.float32(slope) * pos))
    k = np.zeros((MROW - 48, TP), np.float32)
    k[0:2], k[2:4] = pos, 1
    return q, k


def kernel(x, L0_tok_W1, L0_tok_b1, L0_tok_W2, L0_tok_b2, L0_tok_ln1_g, L0_tok_ln1_b, L0_tok_ln2_g,
           L0_tok_ln2_b, L0_tok_Wq, L0_tok_bq, L0_tok_Wk, L0_tok_bk, L0_tok_Wv, L0_tok_bv, L0_tok_Wo,
           L0_tok_bo, L0_tok_Fw1, L0_tok_Fb1, L0_tok_Fw2, L0_tok_Fb2, L0_attn_w_in, L0_attn_w_out,
           L0_ffn_gate_w, L0_ffn_expert_w):
    import concourse.bacc as bacc
    from concourse.bass_utils import run_bass_kernel_spmd

    def turned(a):
        a = np.asarray(a)
        n, k = a.shape
        p = min(k, 128)
        return np.ascontiguousarray(a.T.reshape(k // p, p, n).transpose(1, 0, 2))

    def cols(a):
        return np.asarray(a).reshape(-1, 128).T

    arrays = {"xT": np.zeros((NB + LANES, 128, KT * T), np.float32),
              "W1": turned(L0_tok_W1), "W2": turned(L0_tok_W2)}
    arrays["xT"][:NB] = np.asarray(x).reshape(NB, T, KT, 128).transpose(0, 3, 2, 1).reshape(NB, 128, KT * T)
    for n in (0, 1):
        arrays[f"qkv{n}"] = turned(np.concatenate([L0_tok_Wq[n], L0_tok_Wk[n], L0_tok_Wv[n]]))
        arrays[f"o{n}"] = turned(L0_tok_Wo[n])
        arrays[f"f1{n}"] = turned(L0_tok_Fw1[n])
        arrays[f"f2{n}"] = turned(L0_tok_Fw2[n])
    arrays["qkv2"], arrays["o2"] = turned(L0_attn_w_in), turned(L0_attn_w_out)
    arrays["gate"] = turned(L0_ffn_gate_w)
    arrays["exp"] = turned(np.asarray(L0_ffn_expert_w).reshape(NE * D, D))

    vec = np.zeros((128, 32), np.float32)
    vec[:, 0:4] = cols(L0_tok_b1)
    vec[:, 4:8], vec[:, 8:12] = cols(L0_tok_ln1_g), cols(L0_tok_ln1_b)
    vec[:, 12:16], vec[:, 16:20] = cols(L0_tok_ln2_g), cols(L0_tok_ln2_b)
    for n in (0, 1):
        vec[:, 20 + 4 * n:22 + 4 * n], vec[:, 22 + 4 * n:24 + 4 * n] = cols(L0_tok_bq[n]), cols(L0_tok_bk[n])
        vec[0:FH, 28 + n] = L0_tok_Fb1[n]
    arrays["vec"] = vec
    arrays["row"] = np.stack([np.asarray(a) for a in (
        L0_tok_b2, L0_tok_bo[0], L0_tok_bo[1], L0_tok_Fb2[0], L0_tok_Fb2[1], L0_tok_bv[0], L0_tok_bv[1])])
    arrays["rank"] = np.tile(np.arange(NE, 0, -1, dtype=np.float32), (NT, 1))
    arrays["alibi_q"], arrays["alibi_k"] = alibi_rows()

    nc = bacc.Bacc("TRN2", target_bir_lowering=False, num_devices=1, dynamic_dma_scratch_size=1024)
    ap = {k: nc.dram_tensor(k + "_dram", a.shape, F32, kind="ExternalInput").ap() for k, a in arrays.items()}
    out = nc.dram_tensor("out_dram", (NB, T, D), F32, kind="ExternalOutput").ap()
    tower_kernel(nc, ap["xT"], ap, ap, ap["alibi_q"], ap["alibi_k"], out)
    r = run_bass_kernel_spmd(nc, [{k + "_dram": a for k, a in arrays.items()}], core_ids=[0])
    return r.results[0]["out_dram"]
```

```python
from contextlib import ExitStack

import numpy as np
import concourse.bass as bass
from concourse import mybir

F32 = mybir.dt.float32
F32R = mybir.dt.float32r
BF16 = mybir.dt.bfloat16
ALU = mybir.AluOpType
ACT = mybir.ActivationFunctionType
AX = mybir.AxisListType

NB, S, DIN = 16, 750, 128
T = S // 2
TP = T + 1
TT = 125
NT = T // TT
D = 256
KT = D // 128
DFF, FH = 512, 64
MT = DFF // 128
NE = 8
EPS_TOK, EPS_FIN = 1e-12, 1e-5
MASKED = -1e30
EXP_LN_SET = 6
NCONST = 30
LANES = 2
SLOTS = 3
TURNS = NB // LANES
FIN = 2
HD = {0: 32, 1: 32, FIN: 16}
GROUPS = {0: 2, 1: 2, FIN: 4}
ALI_ROWS = 16 + 4
MROW = {0: 96, 1: 96, FIN: 64}
SCALE = {0: 32 ** -0.5, 1: 32 ** -0.5, FIN: 16 ** -0.5}

WCOL = {}
_at = 0
for _name, _kt, _n, _rows in (
        [("W1", KT, DFF, 128), ("W2", MT, D, 128)]
        + [x for n in (0, 1) for x in ((f"qkv{n}", KT, 3 * D, 128), (f"o{n}", KT, D, 128),
                                       (f"f1{n}", KT, FH, 128), (f"f2{n}", 1, D, FH))]
        + [("qkv2", KT, 3 * D, 128), ("o2", KT, D, 128), ("gate", KT, NE, 128),
           ("exp", KT, NE * D, 128)]):
    WCOL[_name] = (_at, _kt, _n, _rows)
    _at += _kt * _n
WCOLS = _at


OWNER = {
    "g_full": "pe",
    "s_full": "pe", "t_full": "pe",
    "o_full": "pe",
    "s_max": "dve",
    "exp": "act",
    "causal": "pool",
    "x_in0": "sp", "x_in1": "sp", "x_hi": "act", "x_lo": "pool",
    "r_done": "dve", "r_hi": "act", "r_lo": "pool",
    "hi": "act", "lo": "dve",
    "v_done": "dve", "vf_done": "act", "v_zero": "pool",
    "x_done": "dve",
    "scr00": "sp", "scr01": "sp", "scr10": "sp", "scr11": "sp",
    "st_in0": "sp", "st_in1": "sp", "st_in2": "sp",
    "nm_row": "act",
    "ln_st": "dve", "ln_mv": "dve", "ln_log": "act", "ln_rstd": "act", "h_done": "dve",
    "x_bias": "pool", "z_done": "pool",
    "sc_done": "act",
    "gate": "dve", "hot": "dve", "den": "act", "out0": "sp", "out1": "sp"}


HALVED = ("up", "down", "qkv", "wo", "moe", "pv")


UNITS = LANES * sum(GROUPS.values())


def slot(k):
    return 1 if k == UNITS - 1 and UNITS % SLOTS == 1 else k % SLOTS


def lane_steps(l):
    out = []

    def add(step, *needs):
        if step[0] in HALVED:
            out.append((("pre", l, step), needs))
            needs = (("pre", l, step),)
        out.append((step, needs))
        return step

    p = add(("xin", l))
    for m in range(MT):
        h = add(("up", l, m), p)
    for i in range(NT):
        p = add(("down", l, i), h)
    p = add(("lnv", l, 0, 0), p)
    for n in (0, 1, FIN):
        p = add(("lna", l, n, 0), p)
        p = add(("lnt", l, n, 0), p)
        s = {}
        for m in (0, 2, 1, 3):
            q = add(("qkv", l, n, m), p)
            s[m % 2] = add(("spill", l, n, m), q)
        for i in range(NT):
            v = add(("qkv", l, n, 4 + i), p)
        for g in range(GROUPS[n]):
            u = (l, n, g)
            f = add(("fill", u), s[g * 2 // GROUPS[n]])
            for j in range(4):
                for i in range(NT):
                    m = add(("S", u, j, i), f)
            m = add(("nm", u), m)
            for kt in range(NT):
                for j in range(4):
                    t = add(("T", u, kt, j), m)
                pv = add(("pv", u, kt), t, v)
            if n != FIN or g % 2:
                o = add(("sums", u), pv)
                o = add(("norm", u), o)
        if n == FIN:
            add(("xload", l), pv)
        for i in range(NT):
            p = add(("wo", l, n, i), o)
        p = add(("lnv", l, n, 1), p)
        p = add(("lna", l, n, 1), p)
        p = add(("lnt", l, n, 1), p)
        if n != FIN:
            p = add(("f1", l, n), p)
            for i in range(NT):
                h = add(("f2", l, n, i), p)
            p = add(("lnv", l, n + 1, 0), h)
    p = add(("score", l), p)
    p = add(("gate", l), p)
    for i in range(NT):
        for e in range(NE // 2):
            h = add(("moe", l, i, e), p)
    add(("out", l), h)
    return out


def cost(step):
    if step[0] == "pre":
        return (cost_whole(step[2])[0] / 2,)
    pe, *rest = cost_whole(step)
    return (pe / 2 if step[0] in HALVED else pe, *rest)


def cost_whole(step):
    k = step[0]
    fin = (step[1][1] if isinstance(step[1], tuple) else step[2] if len(step) > 2 else 0) == FIN
    if k == "qkv":
        return (.95, ("act", .43), ("dve", .5)) if step[3] < 4 else (.65, ("act" if fin else "dve", .33))
    if k in ("S", "T", "pv"):
        part = (step[3] + 1) / 3 if k == "S" and fin else (3 - step[2]) / 3 if fin else 1
        return {"S": (0.03 + .14 * part + .05 * fin, ("dve", .05 + .41 * part)),
                "T": (0.02 + .14 * part, ("act", .05 + .32 * part)), "pv": (0.1 + 1.3 * part,)}[k]
    return {"xin": (0, ("act", .75), ("pool", 1.75)), "up": (.95, ("dve", .51), ("act", .41), ("pool", .93)),
            "down": (1.3, ("dve", .35)), "lnv": (0, ("dve", 1.5), ("act", .35)), "lna": (0, ("dve", 1.1), ("pool", 1.8)),
            "lnt": (.7, ("act", .8), ("dve", .5)), "spill": (0, ("sp", 1.4), ("dma", 2.2)),
            "fill": (0, ("sp", 1.0 if fin else .5), ("dma", 2.8)), "nm": (.1, ("act", 1.3)),
            "sums": (0, ("act", .9)), "norm": (0, ("dve", .46), ("act", .41), ("pool", .93)),
            "xload": (0, ("sp", .5)), "wo": (.65, ("dve", .35)), "f1": (.95, ("dve", .51), ("act", .41), ("pool", .93)),
            "f2": (.35, ("dve", .35)), "score": (1.0, ("act", .4)), "gate": (.15, ("dve", 1.1)), "moe": (1.3, ("dve", .93)),
            "out": (0, ("sp", .7))}[k]


CUT = ("wo", 1, 2, 0)


def order():
    lanes = [lane_steps(0), lane_steps(1)]
    at = [s for s, _ in lanes[1]].index(CUT) - (CUT[0] in HALVED)
    late = {s for s, _ in lanes[1][at:]}
    lanes[1] = lanes[1][at:] + lanes[1][:at]
    needs, behind, tracks = {}, {}, {}
    for l, steps in enumerate(lanes):
        names = [s for s, _ in steps]
        for p, (s, need) in enumerate(steps):
            needs[s] = [x for x in need if names.index(x) < p]
            if s[0] == "xin" and p:
                needs[s] = [names[p - 1]]
            k = s[2][0] if s[0] == "pre" else s[0]
            tracks.setdefault((l, {"fill": "s", "S": "s", "nm": "s", "T": "t", "pv": "t"}.get(k)), []).append(s)
        load = 0
        for s in reversed(names):
            load += W_LOAD * cost(s)[0]
            behind[s] = max(load, sum([cost(s)[0]] + [d for _, d in cost(s)[1:]]) + max(
                [behind[x] for x in behind if s in needs[x]], default=0))
    free = dict(pe=0, act=0, dve=0, pool=0, sp=0)
    spans, warm, window = [], True, 0
    bank = {"g": [0, 0], "S": [0, 0], "T": [0, 0]}
    done, units, out, opened = {}, [], [], None

    def start(s):
        k, u = s[:2]
        pre = k == "pre"
        wait = list(needs[s])
        if any(x not in done for x in wait):
            return None
        if pre:
            k, u = s[2][:2]
        if opened and cost(s)[0] and k not in ("S", "T", "pv") and s != opened:
            return None
        if k == "fill" and units:
            v = units[-1]
            if v[1] == FIN and v[2] % 2 == 0 and u != (v[0], FIN, v[2] + 1):
                return None
            last = [v for n, v in enumerate(units) if slot(n) == slot(len(units))]
            if last:
                wait.append(("T", last[-1], NT - 1, 3))
        if k in ("T", "pv") and units.index(u):
            v = units[units.index(u) - 1]
            if k == "T":
                wait.append(("pv", v, s[2]))
            elif pre and s[2][2] == 0 and ("norm", v) in needs:
                wait.append(("norm", v))
        if any(x not in done for x in wait):
            return None
        t = max([HAND / 2 + done[x] - (1.6 if x[0] == "norm" and k == "pv" else 1.8 if x[0] == "lna" else 0) + (
            .9 if k == "pv" and x[0] == "T" and u[1] == FIN else 0) for x in wait], default=0)
        if cost(s)[0]:
            t = max(t, free["pe"], 0 if k == "pv" or s == opened else bank.get(k, bank["g"])[0] + HAND / 2)
        return t

    while any(tracks.values()):
        ready = [(start(q[0]), q) for q in tracks.values() if q and start(q[0]) is not None]
        first = min(t for t, _ in ready)
        t, q = min(((t, q) for t, q in ready if t <= first + NEAR), key=lambda x: -behind[x[1][0]] - URGENT.get(x[1][0][2][0] if x[1][0][0] == "pre" else x[1][0][0], 0))
        s = q.pop(0)
        k, (pe, *rest) = s[0], cost(s)
        while t > (window + 1) * HAM:
            used = sum(max(0, min(b, (window + 1) * HAM) - max(a, window * HAM)) for a, b in spans[-60:]) / HAM
            warm, window = used > (.43 if warm else .87), window + 1
        pe *= 1 if warm else 2
        if pe:
            spans.append((t, t + pe))
        end = t + pe
        for e, d in rest:
            end = max(end + HAND, free.get(e, 0)) + d
            if e != "dma":
                free[e] = end
        if pe:
            free["pe"] = t + pe
            if k == "pre":
                opened = s[2] if s[2][0] != "pv" else opened
            elif k != "pv":
                opened = None if s == opened else opened
                b = bank.get(k, bank["g"])
                b[:] = [b[1], t + pe + .5 if k in ("up", "f1") else end]
        if k == "fill":
            units.append(s[1])
        done[s] = end
        out.append(s)
    return out, late


W_LOAD, HAND, NEAR = 0.96, .17, 0.27
HAM = 3.413
URGENT = {"T": 23, "qkv": -7, "lnt": 9, "moe": -18, "up": 5, "down": 6, "f1": 14,
          "wo": -19, "nm": -8, "f2": 11, "gate": 7, "S": 4, "lna": -2}
ORDER, LATE = order()


class Count:

    def __init__(self):
        self.total, self.after, self.spot, self.by_step = 0, {}, {}, {}

    def add(self, key, n, spot, step):
        self.total += n
        self.after[key], self.spot[key] = self.total, spot
        self.by_step[step] = self.by_step.get(step, 0) + n


def tower_kernel(nc, xT, w, small, alibi, out):
    with ExitStack() as ctx:
        def sb(name, shape, dt):
            return ctx.enter_context(nc.sbuf_tensor(name, shape, dt))

        def bank(name):
            return ctx.enter_context(nc.psum_tensor(name, [128, 512], F32))

        def sem(name):
            return ctx.enter_context(nc.semaphore(name))

        w_hi, w_lo = sb("w_hi", [128, WCOLS], F32R), sb("w_lo", [128, WCOLS], F32R)
        xres = [sb(f"xres{l}", [128, NT, D], F32) for l in range(LANES)]
        hv = [sb(f"hv{l}", [128, 6 * D], F32) for l in range(LANES)]
        a_hi = [sb(f"a_hi{l}", [128, KT, TP], F32R) for l in range(LANES)]
        a_lo = [sb(f"a_lo{l}", [128, KT, TP], F32R) for l in range(LANES)]
        b_hi = [sb(f"b_hi{l}", [128, MT, TP], F32R) for l in range(LANES)]
        b_lo = [sb(f"b_lo{l}", [128, MT, TP], F32R) for l in range(LANES)]
        qk_st = [sb(f"qk_st{s}", [128, 2, 4, TP], F32R) for s in range(SLOTS)]
        q_st, k_st = [t[:, 0] for t in qk_st], [t[:, 1] for t in qk_st]
        pt = sb("pt", [128, 4, NT, TP], F32)
        rt = [sb(f"rt{s}", [128, TP], F32) for s in range(2)]
        rden = sb("rden", [128, T], F32)
        nmx = [sb(f"nmx{s}", [128, 12], F32) for s in range(SLOTS)]
        scr = [nc.dram_tensor(f"scr_{l}", [2, 3, 32, 2, 4, TP], F32, kind="Internal").ap() for l in range(LANES)]
        ali = nc.dram_tensor("ali", [4, ALI_ROWS, 2 * 4 * TP], F32, kind="Internal").ap()
        stats = sb("stats", [128, LANES, NT, 6], F32)
        mv = sb("mv", [128, LANES, NT, 2], F32)
        lnv_t = sb("lnv_t", [128, LANES, NT], F32)
        rstd = sb("rstd", [128, LANES, NT], F32)
        gmax = sb("gmax", [128, LANES, 2, NT], F32)
        geq = sb("geq", [128, LANES, NT, NE], F32)
        sc_t = sb("sc_t", [NE, TP], F32)
        hot = sb("hot", [128, LANES, NT, NE], F32)
        rank = sb("rank", [128, NT, NE], F32)
        ident = sb("ident", [128, 128], F32)
        ident_b = sb("ident_b", [128, 128], BF16)
        mask_b = sb("mask_b", [128, TT], BF16)
        ones_pv = sb("ones_pv", [128, 3, 32], F32)
        vec = sb("vec", [128, 32], F32)
        lnb_b = xres[0][:].rearrange("p i d -> p (i d)")[:, 0:2 * KT * TT].rearrange(
            "p (n k t) -> p n k t", n=2, k=KT)
        row = sb("row", [128, 7, D], F32)
        bias_qk = sb("bias_qk", [128, 2, 4], F32)
        bias_f1 = sb("bias_f1", [64, 2], F32)
        stage = [pt[:].rearrange("p a b c -> p (a b c)")[:, 2048 * s:2048 * s + 2048] for s in range(2)]

        ali_in = pt[0:4 * ALI_ROWS].rearrange("p a b c -> p (a b c)")[:, 0:2 * 4 * TP]
        ali_st = qk_st[0][0:4 * ALI_ROWS].rearrange("p x j t -> p (x j t)")

        ps_g = [bank(f"ps_g{i}") for i in range(2)]
        ps_s = [bank(f"ps_s{i}") for i in range(2)]
        ps_t = [bank(f"ps_t{i}") for i in range(2)]
        ps_o, ps_d = bank("ps_o"), bank("ps_d")

        V_B1, V_G1, V_H1, V_G2, V_H2, V_BQ, V_F1 = 0, 4, 8, 12, 16, 20, 28
        R_B2, R_BO, R_F2, R_BV = 0, 1, 3, 5

        def v_view(l):
            return hv[l][0:TT].rearrange("p (k r a s d) -> p k r a s d", k=NT, r=2, s=2, d=16)

        def wslice(t, name, kt, lo, hi):
            at, _, n, rows = WCOL[name]
            return t[0:rows, at + kt * n + lo:at + kt * n + hi]

        c = {x: Count() for x in OWNER}
        g_use, rt_use = {}, {}
        g_reader, rt_user = [], []
        unit_slot, units = {}, []
        for spot, step in enumerate(ORDER):
            st, l = step[0], step[1]

            def add(name, key, n=1):
                c[name].add(key, n, spot, step)

            def use_bank(k, by, key):
                g_use[step, k] = len(g_reader)
                g_reader.append((by, key))
                add("g_full", (step, k))

            def split_rt():
                rt_use[step] = len(rt_user)
                rt_user.append(step)
                for x in ("r_done", "r_hi", "r_lo"):
                    add(x, step)

            if st == "xload":
                add(f"x_in{l}", step, 16)
            if st == "xin":
                add("x_hi", step)
                add("x_lo", step)
            if st in ("up", "f1"):
                use_bank(0, "r_done", step)
                split_rt()
            if st == "lnt" or st == "qkv" and step[3] < 4:
                for k in range(KT if st == "lnt" else 1):
                    use_bank(k, "lo", (step, k))
                    add("hi", (step, k))
                    add("lo", (step, k))
            if st == "qkv" and step[3] == 3 and step[2] == FIN:
                add("v_zero", step, 2)
            if st == "qkv" and step[3] >= 4:
                by = "vf_done" if step[2] == FIN else "v_done"
                use_bank(0, by, step)
                add(by, step, 2 if step[2] == FIN else 1)
            if st == "spill":
                add(f"scr{l}{step[3] % 2}", step, 16 * 3)
            if st in ("down", "wo", "f2"):
                use_bank(0, "x_done", step)
                add("x_done", step)
            if st == "moe":
                use_bank(0, "x_done", (step, 1))
                add("x_done", (step, 0))
                add("x_done", (step, 1))
            if st == "out":
                add(f"out{l}", step, 16)
            if st == "fill":
                u = step[1]
                unit_slot[u] = slot(len(units))
                units.append(u)
                add(f"st_in{unit_slot[u]}", u, 16 * (2 if u[1] == FIN else 1))
            if st == "S":
                add("s_full", step[1:])
                add("s_max", step[1:])
            if st == "nm":
                use_bank(0, "nm_row", (step[1], 1))
                add("nm_row", (step[1], 0))
                add("nm_row", (step[1], 1))
            if st == "T":
                add("t_full", step[1:])
                add("exp", step[1:])
                if step[1][1] == FIN and step[3] == 3:
                    add("causal", step[1:3])
            if st == "pv":
                add("o_full", step[1:])
            if st == "sums":
                add("den", (step, 0))
                add("den", (step, 1))
            if st == "norm":
                split_rt()
            if st == "lnv":
                add("ln_st", step, NT)
                add("ln_mv", step, NT)
                add("ln_log", step)
                add("ln_rstd", step)
            if st == "lna":
                add("h_done", step, NT)
                if step[2:] == (FIN, 1):
                    add("z_done", l)
                elif step[2] != FIN:
                    add("x_bias", step)
            if st == "score":
                use_bank(0, "sc_done", step)
                add("sc_done", step)
            if st == "gate":
                use_bank(0, "gate", (step, 2))
                for k in (1, 2, 3, 4):
                    add("gate", (step, k))
                add("hot", step)
        assert len(g_reader) % 2 == len(rt_user) % 2 == 0 and len(units) == UNITS
        slot_before = {u: [v for v in units[k:] + units[:k] if unit_slot[v] == unit_slot[u]][-1]
                       for k, u in enumerate(units)}
        norms = [i for i in ORDER if i[0] == "norm"]
        s_uses, t_uses = list(c["s_max"].after), list(c["exp"].after)
        sems = {x: sem(x) for x in c}
        zeroed, zeroed_p, loaded0, loaded1, split_hi, split_lo, consts, ident_ok, alibi_ok, alibi_in, small_in, bias_mm, bias_ok, ready = (sem(x) for x in (
            "zeroed", "zeroed_p", "loaded0", "loaded1", "split_hi", "split_lo", "consts", "ident_ok", "alibi_ok", "alibi_in", "small_in", "bias_mm", "bias_ok", "ready"))
        apart = {x: 0 if OWNER[x] == "sp" else 210 * k for k, x in enumerate(OWNER)}
        here = [0]

        def waits(eng, turn):
            def after(name, key):
                behind = 1 if c[name].spot[key] > here[0] else 0
                eng.wait_ge(sems[name], turn * c[name].total + (
                    c[name].total * (1 - behind) + c[name].after[key] + apart[name]))

            def ago(name, keys, key, back):
                after(name, keys[keys.index(key) - back])

            def bank_free(u):
                after(*g_reader[u - 2])
            return after, ago, bank_free

        held = sem("held")

        def credit(eng, name):
            for x in OWNER:
                if OWNER[x] == name and not x.startswith("x_in"):
                    eng.sem_inc(sems[x], c[x].total + apart[x])

        def steps(eng, name, turn):
            owed, level = {}, {x: c[x].total * (turn + 1) for x in OWNER} if isinstance(turn, int) else {}

            def settle(step):
                if owed and name != "sp":
                    eng.drain()
                for x, n in owed.items():
                    if name == "sp":
                        eng.wait_ge(sems[x], level[x])
                    eng.sem_inc(sems[x], n)
                    level[x] += n
                owed.clear()
                for x in level:
                    level[x] += c[x].by_step.get(step, 0)

            for here[0], step in enumerate(ORDER):
                late = step in LATE
                if isinstance(turn, int) and (turn == 0 and late or turn == TURNS and not late):
                    for x in OWNER:
                        if OWNER[x] == name and step in c[x].by_step:
                            owed[x] = owed.get(x, 0) + c[x].by_step[step]
                    continue
                settle(step)
                yield step
            settle(None)

        def turns(eng, body):
            body(0)
            with eng.Fori(1, TURNS) as turn:
                body(turn)
            body(TURNS)

        chunks = [("W1", 0, KT, 0, DFF, None), ("W2", 0, MT, 0, D, None)]
        for n in (0, 1):
            chunks += [(f"qkv{n}", 0, KT, 0, 3 * D, V_G1 + 2 * n), (f"o{n}", 0, KT, 0, D, None),
                       (f"f1{n}", 0, KT, 0, FH, V_G2 + 2 * n), (f"f2{n}", 0, 1, 0, D, None)]
        chunks += [("qkv2", 0, KT, 0, 3 * D, None), ("o2", 0, KT, 0, D, None),
                   ("gate", 0, KT, 0, NE, None)]
        chunks += [("exp", kt, 1, 0, NE * D, None) for kt in range(KT)]

        loaded = [loaded0, loaded1]

        def staged(k):
            name, kt0, kts, lo, hi, _ = chunks[k]
            rows = WCOL[name][3]
            return stage[k % 2][0:rows, 0:kts * (hi - lo)].rearrange("p (k n) -> p k n", k=kts)

        def parts(k):
            name, kt0, kts, lo, hi, g = chunks[k]
            at, _, n, rows = WCOL[name]
            v = [t[0:rows, at + kt0 * n:at + (kt0 + kts) * n].rearrange("p (k n) -> p k n", k=kts)
                 for t in (w_hi, w_lo)]
            if g is None:
                yield staged(k), v[0], v[1], None
            else:
                for kt in range(kts):
                    yield staged(k)[:, kt, :], v[0][:, kt, :], v[1][:, kt, :], vec[0:rows, g + kt:g + kt + 1]

        nparts = [len(list(parts(k))) for k in range(len(chunks))]
        upto = [sum(nparts[:k + 1]) for k in range(len(chunks))]
        biased = [k for k, ch in enumerate(chunks) if ch[5] is not None]

        block = ctx.enter_context(nc.Block())

        @block.sync
        def _(sp):
            sp.dma_start(vec[:], small["vec"]).then_inc(small_in, 16)
            sp.dma_start(row[0:TT], small["row"].partition_broadcast(TT)).then_inc(small_in, 16)
            sp.dma_start(rank[:], small["rank"].partition_broadcast(128)).then_inc(small_in, 16)
            sp.dma_start(ali_in, alibi).then_inc(small_in, 16)
            sp.wait_ge(alibi_ok, 1)
            sp.dma_start(ali.rearrange("g r n -> (g r) n"), ali_st.bitcast(F32)).then_inc(alibi_in, 16)
            for k in range(len(chunks)):
                name, kt0, kts, lo, hi, _ = chunks[k]
                if k >= 2:
                    sp.wait_ge(split_lo, upto[k - 2])
                    nb = len([b for b in biased if b <= k - 2])
                    if nb:
                        sp.wait_ge(bias_mm, nb)
                sp.dma_start(staged(k), w[name][:, kt0:kt0 + kts, :]).then_inc(loaded[k % 2], 16)
            sp.wait_ge(alibi_in, 16)
            sp.sem_inc(ready, 1)
            credit(sp, "sp")
            for l in range(LANES):
                sp.dma_start(hv[l][:, 3 * D:3 * D + KT * T], xT[l]).then_inc(sems[f"x_in{l}"], 16)
            sp.wait_ge(ready, 5)

            def body(turn):
                after, ago, bank_free = waits(sp, turn)
                seq = {}
                for l in range(LANES):
                    for k, ahead in (("xload", 1), ("out", 0)):
                        s = turn * LANES + (LANES * (ahead - ((k, l) in LATE)) + l)
                        seq[k, l] = s if isinstance(turn, int) else sp.snap(s)
                for step in steps(sp, "sp", turn):
                    kind, l = step[0], step[1]
                    if kind == "xload":
                        after("o_full", ((l, FIN, GROUPS[FIN] - 1), NT - 1))
                        sp.dma_start(hv[l][:, 3 * D:3 * D + KT * T], xT[bass.ds(seq[step], 1)].rearrange(
                            "o p n -> (o p) n")).then_inc(sems[f"x_in{l}"], 16)
                    if kind == "spill":
                        _, _, n, m = step
                        half, x = m % 2, m // 2
                        after("lo", (("qkv", l, n, m), 0))
                        for r, part in enumerate((b_hi, b_lo, b_hi) if x == 0 else (b_hi, b_hi, b_lo)):
                            sp.dma_start(scr[l][half, r, :, x].rearrange("p j t -> j p t"),
                                         part[l][:, m, :].bitcast(F32)).then_inc(sems[f"scr{l}{half}"], 16)
                    if kind == "fill":
                        u = l, n, g = step[1]
                        s = unit_slot[u]
                        half = g * 2 // GROUPS[n]
                        if g in (0, GROUPS[n] // 2):
                            after(f"scr{l}{half}", ("spill", l, n, 2 + half))
                            sp.sem_inc(held, 1)
                        after("exp", (slot_before[u], NT - 1, 3))
                        st = qk_st[s][:].rearrange("p x j t -> p (x j t)")
                        dims = slice(0, 32) if n != FIN else slice(16 * (g % 2), 16 * (g % 2) + 16)
                        sp.dma_start(st[0:3 * HD[n]].bitcast(F32),
                                     scr[l][half, :, dims].rearrange("r p x j t -> r p (x j t)")
                                     ).then_inc(sems[f"st_in{s}"], 16)
                        if n == FIN:
                            sp.dma_start(st[3 * HD[n]:MROW[n] + 4].bitcast(F32), ali[g]
                                         ).then_inc(sems[f"st_in{s}"], 16)
                    if kind == "out":
                        after("x_done", (("moe", l, NT - 1, NE // 2 - 1), 1))
                        sp.dma_start(out[bass.ds(seq[step], 1)].rearrange("o (i p) d -> (o p) i d", p=TT),
                                     xres[l][0:TT]).then_inc(sems[f"out{l}"], 16)

            turns(sp, body)
            for l in range(LANES):
                sp.wait_ge(sems[f"out{l}"], 16 * (TURNS + 2))
                sp.wait_ge(sems[f"x_in{l}"], 16 * (TURNS + 2))

        @block.tensor
        def _(pe):
            pe.wait_ge(ident_ok, 3)
            pe.wait_ge(consts, NCONST)
            for b, k in enumerate(biased):
                n, f1 = b // 2, b % 2
                pe.wait_ge(loaded[k % 2], 16 * (k // 2 + 1))
                if b:
                    pe.wait_ge(bias_ok, [2, 3, 5, 6][b - 1])
                src, mm_n = staged(k), FH if f1 else 128
                for m in range(1 if f1 else 4):
                    for kt in range(KT):
                        at = (V_H2 if f1 else V_H1) + 2 * n + kt
                        mm = pe.matmul(ps_g[0][0:mm_n, m:m + 1], src[:, kt, 128 * m:128 * m + mm_n],
                                       vec[:, at:at + 1], start=kt == 0, stop=kt == KT - 1)
                if not f1:
                    for kt in range(KT):
                        mm = pe.matmul(ps_g[1][0:TT, 0:D], lnb_b[:, n, kt, :], src[:, kt, 2 * D:3 * D],
                                       start=kt == 0, stop=kt == KT - 1)
                mm.then_inc(bias_mm, 1)
            credit(pe, "pe")
            pe.drain().then_inc(ready, 1)
            pe.wait_ge(ready, 5)

            def passes(dst, terms, done=None, half=None):
                k, n = 0, 3 * len(terms)
                for st, mv_ in terms:
                    for a, b in ((1, 0), (0, 1), (0, 0)):
                        if half is None or half == 2 * k // n:
                            mm = pe.matmul(dst, st[a], mv_[b], start=k == 0, stop=k == n - 1)
                        k += 1
                if done is not None and half != 0:
                    mm.then_inc(done, 1)

            def wpair(name, kt, lo, hi):
                return wslice(w_hi, name, kt, lo, hi), wslice(w_lo, name, kt, lo, hi)

            def bypart(t, l, kt, lo, hi, rows=128):
                return t[0][l][0:rows, kt, lo:hi], t[1][l][0:rows, kt, lo:hi]

            def body(turn):
                after, ago, bank_free = waits(pe, turn)
                AB, BB = (a_hi, a_lo), (b_hi, b_lo)

                for step in steps(pe, "pe", turn):
                    half = None if step[0] not in HALVED and step[0] != "pre" else int(step[0] != "pre")
                    if step[0] == "pre":
                        step = step[2]
                    kind, l = step[0], step[1]
                    if (step, 0) in g_use and kind != "nm":
                        u = g_use[step, 0]
                        bank = ps_g[u % 2]
                    if kind == "up":
                        m = step[2]
                        if m == half == 0:
                            after("x_lo", ("xin", l))
                        if half == 0:
                            bank_free(u)
                        passes(bank[:, 0:TP], [(wpair("W1", kt, 128 * m, 128 * m + 128),
                                                bypart(AB, l, kt, 0, TP)) for kt in range(KT)], sems["g_full"], half)
                    if kind == "down":
                        i = step[2]
                        if i == half == 0:
                            after("r_lo", ("up", l, MT - 1))
                        if half == 0:
                            bank_free(u)
                        passes(bank[0:TT, 0:D], [(bypart(BB, l, kt, TT * i, TT * i + TT), wpair("W2", kt, 0, D))
                                                 for kt in range(MT)], sems["g_full"], half)
                    if kind == "lnt":
                        after("h_done", ("lna", *step[1:]))
                        for kt in range(KT):
                            u = g_use[step, kt]
                            bank_free(u)
                            for i in range(NT):
                                mm = pe.transpose(ps_g[u % 2][:, TT * i:TT * i + TT],
                                                  hv[l][0:TT, D * i + 128 * kt:D * i + 128 * kt + 128],
                                                  ident[0:TT, 0:TT])
                            mm.then_inc(sems["g_full"], 1)
                    if kind == "qkv":
                        n, m = step[2:]
                        if m == half == 0:
                            after("lo", (("lnt", l, n, 0), KT - 1))
                        if half == 0:
                            bank_free(u)
                        if m < 4:
                            passes(bank[:, 0:TP], [(wpair(f"qkv{n}", kt, 128 * m, 128 * m + 128),
                                                    bypart(AB, l, kt, 0, TP)) for kt in range(KT)],
                                   sems["g_full"], half)
                        else:
                            i = m - 4
                            passes(bank[0:TT, 0:D], [(bypart(AB, l, kt, TT * i, TT * i + TT),
                                                      wpair(f"qkv{n}", kt, 2 * D, 3 * D)) for kt in range(KT)],
                                   sems["g_full"], half)
                    if kind == "S":
                        su, j, i = step[1:]
                        s, n = unit_slot[su], su[1]
                        b = ps_s[s_uses.index(step[1:]) % 2]
                        if j == i == 0:
                            after(f"st_in{s}", su)
                        ago("s_max", s_uses, step[1:], 2)
                        cols = TP if n != FIN or i == NT - 1 else (TT * (i + 1) + 1) // 2 * 2
                        mm = pe.matmul(b[0:TT, 0:cols], q_st[s][0:MROW[n], j, TT * i:TT * i + TT],
                                       k_st[s][0:MROW[n], j, 0:cols], start=True, stop=n != FIN)
                        if n == FIN:
                            mm = pe.matmul(b[0:TT, TT * i:TT * i + TT], ident_b[0:TT, 0:TT],
                                           mask_b[0:TT, :], start=False, stop=True)
                        mm.then_inc(sems["s_full"], 1)
                    if kind == "nm":
                        un = step[1]
                        u = g_use[step, 0]
                        after("s_max", (un, 3, NT - 1))
                        bank_free(u)
                        at = MROW[un[1]]
                        for i in range(NT):
                            mm = pe.matmul(ps_g[u % 2][at:at + 4, TT * i:TT * i + TT],
                                           nmx[unit_slot[un]][0:TT, 4 * i:4 * i + 4], ident[0:TT, 0:TT],
                                           start=True, stop=True)
                        mm.then_inc(sems["g_full"], 1)
                    if kind == "T":
                        tu, kt, j = step[1:]
                        s, n = unit_slot[tu], tu[1]
                        if kt == 0 and j % 2 == 0:
                            after("nm_row", (tu, j // 2))
                        ago("exp", t_uses, step[1:], 2)
                        q0 = TT * kt // 2 * 2 if n == FIN else 0
                        pe.matmul(ps_t[t_uses.index(step[1:]) % 2][0:TT, 0:TP - q0],
                                  k_st[s][0:MROW[n] + 4, j, TT * kt:TT * kt + TT],
                                  q_st[s][0:MROW[n] + 4, j, q0:TP], start=True, stop=True
                                  ).then_inc(sems["t_full"], 1)
                    if kind == "pv":
                        un, kt = step[1:]
                        l, n, g = un
                        if half == 0:
                            if n == FIN:
                                after("causal", (un, kt))
                            else:
                                after("exp", (un, kt, 3))
                            if g == 0 and kt == 0:
                                after("vf_done" if n == FIN else "v_done", ("qkv", l, n, 3 + NT))
                                if n == FIN:
                                    after("v_zero", ("qkv", l, n, 3))
                        first, final = (g % 2 == 0, g % 2 == 1) if n == FIN else (True, True)
                        if first and kt == half == 0:
                            norm = ("norm", (l, n, g + (n == FIN)))
                            ago("r_done", norms, norm, 1)
                        q0 = TT * kt if n == FIN else 0
                        for j in range(4) if half == 0 else ():
                            if n == FIN:
                                at = 512 * kt + 256 * (g % 2) + 128 * (g // 2) + 32 * j
                            else:
                                at = 3 * D + D * kt + 128 * g + 32 * j
                            pe.matmul(ps_o[32 * j:32 * j + 32, q0:T], hv[l][0:TT, at:at + 32],
                                      pt[0:TT, j, kt, q0:T], start=first and kt == 0,
                                      stop=final and kt == NT - 1)
                        for j in range(4) if half == 1 else ():
                            mm = pe.matmul(ps_d[32 * j:32 * j + 32, q0:T],
                                           ones_pv[0:TT, 1 + g % 2 if n == FIN else 0, :],
                                           pt[0:TT, j, kt, q0:T], start=first and kt == 0,
                                           stop=final and kt == NT - 1)
                        if half == 1:
                            mm.then_inc(sems["o_full"], 1)
                    if kind == "wo":
                        n, i = step[2:]
                        if i == half == 0:
                            after("r_lo", ("norm", (l, n, GROUPS[n] - 1)))
                        if half == 0:
                            bank_free(u)
                        passes(bank[0:TT, 0:D], [(bypart(AB, l, kt, TT * i, TT * i + TT),
                                                  wpair(f"o{n}", kt, 0, D)) for kt in range(KT)], sems["g_full"], half)
                    if kind == "f1":
                        n = step[2]
                        after("lo", (("lnt", l, n, 1), KT - 1))
                        bank_free(u)
                        passes(bank[0:FH, 0:TP], [(wpair(f"f1{n}", kt, 0, FH), bypart(AB, l, kt, 0, TP))
                                                  for kt in range(KT)], sems["g_full"])
                    if kind == "f2":
                        n, i = step[2:]
                        if i == 0:
                            after("r_lo", ("f1", l, n))
                        bank_free(u)
                        passes(bank[0:TT, 0:D], [(bypart(BB, l, 0, TT * i, TT * i + TT, FH),
                                                  wpair(f"f2{n}", 0, 0, D))], sems["g_full"])
                    if kind == "score":
                        after("lo", (("lnt", l, FIN, 1), KT - 1))
                        bank_free(u)
                        passes(bank[0:NE, 0:TP], [(wpair("gate", kt, 0, NE), bypart(AB, l, kt, 0, TP))
                                                  for kt in range(KT)], sems["g_full"])
                    if kind == "gate":
                        after("sc_done", ("score", l))
                        bank_free(u)
                        for i in range(NT):
                            mm = pe.matmul(bank[0:TT, NE * i:NE * i + NE], sc_t[:, TT * i:TT * i + TT],
                                           ident[0:NE, 0:NE], start=True, stop=True)
                        mm.then_inc(sems["g_full"], 1)
                    if kind == "moe":
                        i, e = step[2:]
                        if half == 0:
                            bank_free(u)
                        passes(bank[0:TT, :], [(bypart(AB, l, kt, TT * i, TT * i + TT),
                                                wpair("exp", kt, 2 * e * D, 2 * (e + 1) * D))
                                               for kt in range(KT)], sems["g_full"], half)

            turns(pe, body)

        @block.scalar
        def _(act):
            act.add_instruction(mybir.InstLoadActFuncSet(name=nc.get_next_instruction_name(),
                                                         act_func_set_id=EXP_LN_SET, ins=[], outs=[]))
            act.wait_ge(small_in, 16 * 4)
            act.copy(ali_st, ali_in).then_inc(alibi_ok, 1)
            for k in range(len(chunks)):
                act.wait_ge(loaded[k % 2], 16 * (k // 2 + 1))
                for src, hi, _, g in parts(k):
                    if g is None:
                        act.copy(hi, src).then_inc(split_hi, 1)
                    else:
                        act.activation(hi, src, ACT.Copy, scale=g).then_inc(split_hi, 1)
            credit(act, "act")
            act.drain().then_inc(ready, 1)
            act.wait_ge(ready, 5)

            def body(turn):
                after, ago, bank_free = waits(act, turn)
                for step in steps(act, "act", turn):
                    kind, l = step[0], step[1]
                    if kind == "xin":
                        after(f"x_in{l}", ("xload", l))
                        after("g_full", (("moe", l, NT - 1, NE // 2 - 1), 0))
                        act.copy(a_hi[l][:, :, 0:T], hv[l][:, 3 * D:3 * D + KT * T].rearrange(
                            "p (k t) -> p k t", k=KT)).then_inc(sems["x_hi"], 1)
                    if kind == "sums":
                        after("o_full", (step[1], NT - 1))
                        act.activation(rden[:], ps_d[:, 0:T], ACT.Ln).then_inc(sems["den"], 1)
                        after("den", (step, 0))
                        ago("r_done", norms, ("norm", step[1]), 1)
                        act.activation(rden[:], rden[:], ACT.Exp, scale=-1.0).then_inc(sems["den"], 1)
                    if step in rt_use:
                        if kind == "norm":
                            l, n, g = step[1]
                            dst = a_hi[l][:, g // 2 if n == FIN else g, 0:T]
                        else:
                            dst = b_hi[l][:, step[2], 0:T] if kind == "up" else b_hi[l][0:FH, 0, 0:T]
                        after("r_done", step)
                        act.copy(dst, rt[rt_use[step] % 2][0:dst.shape[0], 0:T]).then_inc(sems["r_hi"], 1)
                    if kind == "lnt" or kind == "qkv" and step[3] < 4:
                        for k in range(KT if kind == "lnt" else 1):
                            after("g_full", (step, k))
                            src = ps_g[g_use[step, k] % 2][:, 0:T]
                            if kind == "lnt":
                                act.copy(a_hi[l][:, k, 0:T], src).then_inc(sems["hi"], 1)
                            elif step[2] == FIN:
                                act.copy(b_hi[l][:, step[3], 0:T], src).then_inc(sems["hi"], 1)
                            else:
                                m = step[3]
                                act.activation(b_hi[l][:, m, 0:T], src, ACT.Identity,
                                               bias=bias_qk[:, step[2], m:m + 1]).then_inc(sems["hi"], 1)
                    if kind == "qkv" and step[2] == FIN and step[3] >= 4:
                        after("g_full", (step, 0))
                        src = ps_g[g_use[step, 0] % 2][0:TT, 0:D].rearrange("p (a s d) -> p a s d", s=2, d=16)
                        for r in range(2):
                            act.copy(v_view(l)[:, step[3] - 4, r, :, r, :], src[:, :, r, :]).then_inc(sems["vf_done"], 1)
                    if kind == "nm":
                        un = step[1]
                        after("g_full", (step, 0))
                        at = MROW[un[1]]
                        for j in (0, 2):
                            act.copy(q_st[unit_slot[un]][at:at + 4, j:j + 2, 0:T],
                                     ps_g[g_use[step, 0] % 2][at:at + 4, None, 0:T].to_broadcast([4, 2, T])
                                     ).then_inc(sems["nm_row"], 1)
                    if kind == "score":
                        after("g_full", (step, 0))
                        after("hot", ("gate", 1 - l))
                        act.copy(sc_t[:, 0:T], ps_g[g_use[step, 0] % 2][0:NE, 0:T]).then_inc(sems["sc_done"], 1)
                    if kind == "T":
                        un, kt, j = step[1:]
                        n = un[1]
                        after("t_full", step[1:])
                        if j == 0:
                            ago("o_full", [(x, kt) for x in units], (un, kt), 1)
                        q0 = TT * kt if n == FIN else 0
                        b = ps_t[t_uses.index(step[1:]) % 2]
                        act.activation(pt[0:TT, j, kt, q0:T], b[0:TT, q0 % 2:q0 % 2 + T - q0],
                                       ACT.Exp, scale=SCALE[n]).then_inc(sems["exp"], 1)
                    if kind == "lnv":
                        after("ln_mv", step)
                        act.activation(lnv_t[0:TT, l, :], mv[0:TT, l, :, 1], ACT.Ln,
                                       bias=EPS_FIN if step[2] == FIN else EPS_TOK).then_inc(sems["ln_log"], 1)
                        after("ln_log", step)
                        act.activation(rstd[0:TT, l, :], lnv_t[0:TT, l, :], ACT.Exp,
                                       scale=-0.5).then_inc(sems["ln_rstd"], 1)

            turns(act, body)

        @block.vector
        def _(dve):
            for l in range(LANES):
                for t in (a_hi, a_lo, b_hi, b_lo):
                    dve.memset(t[l][:, :, T:TP].bitcast(F32), 0.0).then_inc(consts, 1)
            for s in range(SLOTS):
                dve.memset(q_st[s][MROW[0]:MROW[0] + 4].bitcast(F32), 0.0).then_inc(consts, 1)
            dve.wait_ge(ident_ok, 3)
            for s in range(SLOTS):
                for j in range(4):
                    dve.tensor_copy(k_st[s][MROW[0]:MROW[0] + 4, j, :],
                                    ident[MROW[0]:MROW[0] + 4, MROW[0] + j:MROW[0] + j + 1].to_broadcast([4, TP])
                                    ).then_inc(consts, 1)
            dve.memset(ones_pv[:], 0.0).then_inc(zeroed, 1)
            dve.wait_ge(zeroed, 1)
            dve.memset(ones_pv[:, 0, :], 1.0).then_inc(consts, 1)
            for r in range(2):
                dve.memset(ones_pv[:, 1 + r, 16 * r:16 * r + 16], 1.0).then_inc(consts, 1)
            dve.wait_ge(small_in, 16 * 4)
            for n in range(2):
                for kt in range(KT):
                    at = V_H1 + 2 * n + kt
                    if n == kt == 0:
                        dve.memset(lnb_b, 0.0).then_inc(zeroed, 1)
                        dve.wait_ge(zeroed, 2)
                    dve.tensor_scalar(lnb_b[:, n, kt, :], lnb_b[:, n, kt, :], vec[:, at:at + 1], None, ALU.add
                                      ).then_inc(consts, 1)
            done = 0
            for k in range(len(chunks)):
                for src, hi, lo, g in parts(k):
                    done += 1
                    dve.wait_ge(split_hi, done)
                    if g is None:
                        dve.tensor_tensor(lo, src, hi.bitcast(F32), ALU.subtract).then_inc(split_lo, 1)
                    else:
                        dve.scalar_tensor_tensor(out=lo, in0=src, scalar=g, in1=hi.bitcast(F32),
                                                 op0=ALU.mult, op1=ALU.subtract).then_inc(split_lo, 1)
                if k in biased:
                    b = biased.index(k)
                    n, f1 = b // 2, b % 2
                    dve.wait_ge(bias_mm, b + 1)
                    if f1:
                        dve.tensor_tensor(bias_f1[:, n:n + 1], ps_g[0][0:FH, 0:1], vec[0:FH, V_F1 + n:V_F1 + n + 1],
                                          ALU.add).then_inc(bias_ok, 1)
                    else:
                        dve.tensor_tensor(bias_qk[:, n, :], ps_g[0][:, 0:4], vec[:, V_BQ + 4 * n:V_BQ + 4 * n + 4],
                                          ALU.add).then_inc(bias_ok, 1)
                        dve.tensor_tensor(row[0:TT, R_BV + n, :], ps_g[1][0:TT, 0:D], row[0:TT, R_BV + n, :],
                                          ALU.add).then_inc(bias_ok, 1)
            credit(dve, "dve")
            dve.drain().then_inc(ready, 1)
            dve.wait_ge(ready, 5)

            def body(turn):
                after, ago, bank_free = waits(dve, turn)

                def gbank(step, k=0):
                    after("g_full", (step, k))
                    return ps_g[g_use[step, k] % 2]

                for step in steps(dve, "dve", turn):
                    kind, l = step[0], step[1]
                    if step in rt_use:
                        k = rt_use[step]
                        after("r_lo", rt_user[k - 2])
                        if kind == "norm":
                            after("den", (("sums", step[1]), 1))
                            dve.tensor_tensor(rt[k % 2][:, 0:T], ps_o[:, 0:T], rden[:], ALU.mult
                                              ).then_inc(sems["r_done"], 1)
                        elif kind == "up":
                            m = step[2]
                            dve.tensor_scalar(rt[k % 2][:, 0:T], gbank(step)[:, 0:T],
                                              vec[:, V_B1 + m:V_B1 + m + 1], 0.0, ALU.add, ALU.max
                                              ).then_inc(sems["r_done"], 1)
                        else:
                            dve.tensor_scalar(rt[k % 2][0:FH, 0:T], gbank(step)[0:FH, 0:T],
                                              bias_f1[:, step[2]:step[2] + 1], 0.0, ALU.add, ALU.max
                                              ).then_inc(sems["r_done"], 1)
                    if kind == "down":
                        i = step[2]
                        if i == 0:
                            after(f"out{l}", ("out", l))
                        dve.tensor_tensor(xres[l][0:TT, i, :], gbank(step)[0:TT, 0:D], row[0:TT, R_B2, :],
                                          ALU.add).then_inc(sems["x_done"], 1)
                    if kind in ("wo", "f2"):
                        n, i = step[2:]
                        if n != FIN and i == 0:
                            after("x_bias", ("lna", l, n, int(kind == "f2")))
                        dve.tensor_tensor(xres[l][0:TT, i, :], gbank(step)[0:TT, 0:D], xres[l][0:TT, i, :],
                                          ALU.add).then_inc(sems["x_done"], 1)
                    if kind == "lnv":
                        _, _, n, k2 = step
                        src = ("wo", l, n) if k2 else ("down", l) if n == 0 else ("f2", l, n - 1)
                        after("x_done", (*src, NT - 1))
                        for i in range(NT):
                            dve.bn_stats(stats[0:TT, l, i, :], xres[l][0:TT, i, :]).then_inc(sems["ln_st"], 1)
                        after("ln_st", step)
                        dve.sem_inc(held, 1)
                        for i in range(NT):
                            dve.bn_aggr(mv[0:TT, l, i, :], stats[0:TT, l, i, :]).then_inc(sems["ln_mv"], 1)
                    if kind == "lna":
                        after("ln_rstd", ("lnv", *step[1:]))
                        for i in range(NT):
                            dve.tensor_scalar(hv[l][0:TT, D * i:D * i + D], xres[l][0:TT, i, :],
                                              mv[0:TT, l, i, 0:1], rstd[0:TT, l, i:i + 1],
                                              ALU.subtract, ALU.mult).then_inc(sems["h_done"], 1)
                    if kind == "lnt" or kind == "qkv" and step[3] < 4:
                        for k in range(KT if kind == "lnt" else 1):
                            after("hi", (step, k))
                            src = ps_g[g_use[step, k] % 2][:, 0:T]
                            thi, tlo = (a_hi, a_lo) if kind == "lnt" else (b_hi, b_lo)
                            m = k if kind == "lnt" else step[3]
                            if kind == "qkv" and step[2] != FIN:
                                dve.scalar_tensor_tensor(out=tlo[l][:, m, 0:T], in0=src,
                                                         scalar=bias_qk[:, step[2], m:m + 1],
                                                         in1=thi[l][:, m, 0:T].bitcast(F32), op0=ALU.add,
                                                         op1=ALU.subtract).then_inc(sems["lo"], 1)
                            else:
                                dve.tensor_tensor(tlo[l][:, m, 0:T], src, thi[l][:, m, 0:T].bitcast(F32),
                                                  ALU.subtract).then_inc(sems["lo"], 1)
                    if kind == "qkv" and step[2] != FIN and step[3] >= 4:
                        i = step[3] - 4
                        dve.tensor_tensor(hv[l][0:TT, (3 + i) * D:(4 + i) * D], gbank(step)[0:TT, 0:D],
                                          row[0:TT, R_BV + step[2], :], ALU.add).then_inc(sems["v_done"], 1)
                    if kind == "S":
                        u, j, i = step[1:]
                        s, n = unit_slot[u], u[1]
                        if j == i == 0:
                            after("nm_row", (slot_before[u], 1))
                        after("s_full", step[1:])
                        w = TT * (i + 1) if n == FIN else T
                        dve.tensor_reduce(nmx[s][0:TT, 4 * i + j:4 * i + j + 1],
                                          ps_s[s_uses.index(step[1:]) % 2][0:TT, 0:w],
                                          AX.X, ALU.max, negate=True).then_inc(sems["s_max"], 1)
                    if kind == "gate":
                        def wide(t):
                            return t[:, :, None].to_broadcast([TT, NT, NE])
                        sc = gbank(step)[0:TT, 0:NT * NE].rearrange("p (i e) -> p i e", i=NT)
                        dve.tensor_reduce(gmax[0:TT, l, 0, :], sc, AX.X, ALU.max).then_inc(sems["gate"], 1)
                        after("gate", (step, 1))
                        dve.tensor_tensor(geq[0:TT, l], sc, wide(gmax[0:TT, l, 0, :]), ALU.is_equal
                                          ).then_inc(sems["gate"], 1)
                        after("gate", (step, 2))
                        dve.tensor_tensor(hot[0:TT, l], geq[0:TT, l], rank[0:TT], ALU.mult).then_inc(sems["gate"], 1)
                        after("gate", (step, 3))
                        dve.tensor_reduce(gmax[0:TT, l, 1, :], hot[0:TT, l], AX.X, ALU.max).then_inc(sems["gate"], 1)
                        after("gate", (step, 4))
                        dve.tensor_tensor(hot[0:TT, l], hot[0:TT, l], wide(gmax[0:TT, l, 1, :]), ALU.is_equal
                                          ).then_inc(sems["hot"], 1)
                    if kind == "moe":
                        i, e = step[2:]
                        if i == e == 0:
                            after("z_done", l)
                            after("hot", ("gate", l))
                        bk = gbank(step)
                        for x in range(2):
                            if e or x:
                                after("x_done", (step, 0) if x else ((*step[:3], e - 1), 1))
                            ex = 2 * e + x
                            dve.scalar_tensor_tensor(out=xres[l][0:TT, i, :], in0=bk[0:TT, D * x:D * x + D],
                                                     scalar=hot[0:TT, l, i, ex:ex + 1], in1=xres[l][0:TT, i, :],
                                                     op0=ALU.mult, op1=ALU.add).then_inc(sems["x_done"], 1)

            turns(dve, body)

        @block.gpsimd
        def _(pool):
            for t in (ident, ident_b, mask_b):
                pool.memset(t[:], 0.0).then_inc(zeroed_p, 1)
            pool.wait_ge(zeroed_p, 3)
            for t in (ident, ident_b):
                pool.affine_select(out=t[:], in_=t[:], compare_op=ALU.not_equal, fill=1.0, base=0,
                                   pattern=[[-1, 128]], channel_multiplier=1).then_inc(ident_ok, 1)
            pool.affine_select(out=mask_b[:], in_=mask_b[:], compare_op=ALU.is_ge, fill=MASKED, base=0,
                               pattern=[[-1, TT]], channel_multiplier=1).then_inc(ident_ok, 1)
            credit(pool, "pool")
            pool.drain().then_inc(ready, 1)
            pool.wait_ge(ready, 5)

            def body(turn):
                after, ago, bank_free = waits(pool, turn)
                for step in steps(pool, "pool", turn):
                    kind, l = step[0], step[1]
                    if kind == "xin":
                        after("x_hi", step)
                        pool.tensor_tensor(a_lo[l][:, :, 0:T], hv[l][:, 3 * D:3 * D + KT * T].rearrange(
                            "p (k t) -> p k t", k=KT), a_hi[l][:, :, 0:T].bitcast(F32), ALU.subtract
                            ).then_inc(sems["x_lo"], 1)
                    if step in rt_use:
                        if kind == "norm":
                            l, n, g = step[1]
                            k = g // 2 if n == FIN else g
                            hi, lo = a_hi[l][:, k, 0:T], a_lo[l][:, k, 0:T]
                        else:
                            rows, k = (128, step[2]) if kind == "up" else (FH, 0)
                            hi, lo = b_hi[l][0:rows, k, 0:T], b_lo[l][0:rows, k, 0:T]
                        after("r_hi", step)
                        pool.tensor_tensor(lo, rt[rt_use[step] % 2][0:hi.shape[0], 0:T], hi.bitcast(F32),
                                           ALU.subtract).then_inc(sems["r_lo"], 1)
                    if kind == "lna" and step[2:] != (FIN, 0):
                        _, _, n, k2 = step
                        after("h_done", step)
                        if n == FIN:
                            pool.tensor_tensor(xres[l][0:TT], xres[l][0:TT],
                                               hv[l][0:TT, 0:NT * D].rearrange("p (i d) -> p i d", i=NT), ALU.add
                                               ).then_inc(sems["z_done"], 1)
                        else:
                            at = (R_F2 if k2 else R_BO) + n
                            pool.tensor_tensor(xres[l][0:TT], xres[l][0:TT],
                                               row[0:TT, at:at + 1, :].to_broadcast([TT, NT, D]), ALU.add
                                               ).then_inc(sems["x_bias"], 1)
                    if kind == "qkv" and step[2] == FIN and step[3] == 3:
                        after("hi", (("lnt", l, FIN, 0), KT - 1))
                        pool.sem_inc(held, 1)
                        for r in range(2):
                            pool.memset(v_view(l)[:, :, r, :, 1 - r, :], 0.0).then_inc(sems["v_zero"], 1)
                    if kind == "T" and step[1][1] == FIN and step[3] == 3:
                        kt = step[2]
                        after("exp", step[1:])
                        pool.sem_inc(held, 1)
                        pd = pt[0:TT, :, kt, TT * kt:TT * kt + TT]
                        pool.affine_select(out=pd, in_=pd, compare_op=ALU.is_ge, fill=0.0, base=0,
                                           pattern=[[0, 4], [1, TT]], channel_multiplier=-1
                                           ).then_inc(sems["causal"], 1)

            turns(pool, body)


def alibi_rows():
    def halves(x):
        x = np.float32(x)
        b = x.view(np.uint32)
        hi = ((b + np.uint32(0x7FF) + ((b >> 12) & 1)) & np.uint32(0xFFFFF000)).view(np.float32)
        return hi, np.float32(x - hi)

    pos = np.arange(TP, dtype=np.float32)
    rows = np.zeros((4, ALI_ROWS, 2, 4, TP), np.float32)
    for g in range(4):
        for j in range(4):
            h = 8 * (g // 2) + 2 * j + g % 2
            slope = np.float32(2.0) ** np.float32(-8.0 / 16 * (h + 1)) / np.float32(SCALE[FIN])
            rows[g, 0, 0, j], rows[g, 1, 0, j] = halves(slope)
            rows[g, 2, 0, j], rows[g, 3, 0, j] = halves(-(np.float32(slope) * pos))
            rows[g, 0:2, 1, j], rows[g, 2:4, 1, j] = pos, 1
            rows[g, 16 + j, 1, j] = 1
    return rows.reshape(4 * ALI_ROWS, 2 * 4 * TP)


def kernel(x, L0_tok_W1, L0_tok_b1, L0_tok_W2, L0_tok_b2, L0_tok_ln1_g, L0_tok_ln1_b, L0_tok_ln2_g,
           L0_tok_ln2_b, L0_tok_Wq, L0_tok_bq, L0_tok_Wk, L0_tok_bk, L0_tok_Wv, L0_tok_bv, L0_tok_Wo,
           L0_tok_bo, L0_tok_Fw1, L0_tok_Fb1, L0_tok_Fw2, L0_tok_Fb2, L0_attn_w_in, L0_attn_w_out,
           L0_ffn_gate_w, L0_ffn_expert_w):
    import concourse.bacc as bacc
    from concourse.bass_utils import run_bass_kernel_spmd

    def turned(a):
        a = np.asarray(a)
        n, k = a.shape
        p = min(k, 128)
        return np.ascontiguousarray(a.T.reshape(k // p, p, n).transpose(1, 0, 2))

    def cols(a):
        return np.asarray(a).reshape(-1, 128).T

    arrays = {"xT": np.zeros((NB + LANES, 128, KT * T), np.float32),
              "W1": turned(L0_tok_W1), "W2": turned(L0_tok_W2)}
    arrays["xT"][:NB] = np.asarray(x).reshape(NB, T, KT, 128).transpose(0, 3, 2, 1).reshape(NB, 128, KT * T)
    for n in (0, 1):
        arrays[f"qkv{n}"] = turned(np.concatenate([L0_tok_Wq[n], L0_tok_Wk[n], L0_tok_Wv[n]]))
        arrays[f"o{n}"] = turned(L0_tok_Wo[n])
        arrays[f"f1{n}"] = turned(L0_tok_Fw1[n])
        arrays[f"f2{n}"] = turned(L0_tok_Fw2[n])
    arrays["qkv2"], arrays["o2"] = turned(L0_attn_w_in), turned(L0_attn_w_out)
    arrays["gate"] = turned(L0_ffn_gate_w)
    arrays["exp"] = turned(np.asarray(L0_ffn_expert_w).reshape(NE * D, D))

    vec = np.zeros((128, 32), np.float32)
    vec[:, 0:4] = cols(L0_tok_b1)
    vec[:, 4:8], vec[:, 8:12] = cols(L0_tok_ln1_g), cols(L0_tok_ln1_b)
    vec[:, 12:16], vec[:, 16:20] = cols(L0_tok_ln2_g), cols(L0_tok_ln2_b)
    for n in (0, 1):
        vec[:, 20 + 4 * n:22 + 4 * n], vec[:, 22 + 4 * n:24 + 4 * n] = cols(L0_tok_bq[n]), cols(L0_tok_bk[n])
        vec[0:FH, 28 + n] = L0_tok_Fb1[n]
    arrays["vec"] = vec
    arrays["row"] = np.stack([np.asarray(a) for a in (
        L0_tok_b2, L0_tok_bo[0], L0_tok_bo[1], L0_tok_Fb2[0], L0_tok_Fb2[1], L0_tok_bv[0], L0_tok_bv[1])])
    arrays["rank"] = np.tile(np.arange(NE, 0, -1, dtype=np.float32), (NT, 1))
    arrays["alibi"] = alibi_rows()

    nc = bacc.Bacc("TRN2", target_bir_lowering=False, num_devices=1, dynamic_dma_scratch_size=128)
    ap = {k: nc.dram_tensor(k + "_dram", a.shape, F32, kind="ExternalInput").ap() for k, a in arrays.items()}
    out = nc.dram_tensor("out_dram", (NB, T, D), F32, kind="ExternalOutput").ap()
    tower_kernel(nc, ap["xT"], ap, ap, ap["alibi"], out)
    r = run_bass_kernel_spmd(nc, [{k + "_dram": a for k, a in arrays.items()}], core_ids=[0])
    return r.results[0]["out_dram"]
```
